# Optimizing a Trainium2 kernel written in Bass

```python
import numpy as np
import jax
import jax.numpy as jnp

def _softmax(x, axis=-1):
    return jax.nn.softmax(x, axis=axis)

def _gelu(x):
    return jax.nn.gelu(x, approximate=True)

def _silu(x):
    return jax.nn.silu(x)

def _sigmoid(x):
    return jax.nn.sigmoid(x)

def _layernorm(x, axis=-1, eps=1e-05):
    m = jnp.mean(x, axis=axis, keepdims=True)
    v = jnp.var(x, axis=axis, keepdims=True)
    return (x - m) / jnp.sqrt(v + eps)

def _scatter_add(tgt, idx, src, axis=0):
    return tgt.at[idx].add(src)

def _segment_sum(src, seg, n):
    return jax.ops.segment_sum(src, seg, n)
kernel_name = 'mk_macaron_d1_jaxref_r4_5c4e22'

def setup_inputs(seed: int=0):
    np.random.seed(seed)
    _w = jnp.asarray

    def _L0_attn_setup():
        import jax, jax.numpy as jnp
        import numpy as np
        B, T, HID = (1, 256, 512)
        H, DK, DV, M, KW = (16, 128, 128, 128, 4)
        SCALE = DK ** (-0.5)
        EPS = 1e-05

        def short_conv(x, w):
            K = w.shape[1]
            xp = jnp.pad(x, ((0, 0), (K - 1, 0), (0, 0)))
            t = x.shape[1]
            y = sum((xp[:, i:i + t] * w[:, i] for i in range(K)))
            return jax.nn.silu(y)

        def l2norm(x):
            return x * jax.lax.rsqrt(jnp.sum(x * x, axis=-1, keepdims=True) + 1e-06)

        def gsa2_scan(q, k, v, w, g, beta):
            b = q.shape[0]
            tm = lambda x: jnp.moveaxis(x, 1, 0)
            Sk0 = jnp.zeros((b, H, DK, M), q.dtype)
            Sv0 = jnp.zeros((b, H, M, DV), q.dtype)

            def step(carry, xs):
                Sk, Sv = carry
                q_t, k_t, v_t, w_t, g_t, b_t = xs
                gt = jnp.exp(g_t)
                bw = b_t[:, :, None] * w_t
                Sk = Sk * gt[:, :, None, :] + k_t[..., :, None] * bw[:, :, None, :]
                Sv = Sv * gt[..., None] + bw[..., None] * v_t[:, :, None, :]
                s = jnp.einsum('bhd,bhdm->bhm', q_t, Sk) * SCALE
                a = jax.nn.softmax(s, axis=-1)
                o_t = jnp.einsum('bhm,bhmd->bhd', a, Sv)
                return ((Sk, Sv), o_t)
            (_, _), o = jax.lax.scan(step, (Sk0, Sv0), (tm(q), tm(k), tm(v), tm(w), tm(g), tm(beta)))
            return jnp.moveaxis(o, 0, 1)
        key = jax.random.key(seed)
        ks = jax.random.split(key, 16)
        s = 0.02
        return {'hidden_states': jax.random.normal(ks[0], (B, T, HID), jnp.float32), 'Wq': jax.random.normal(ks[1], (HID, H * DK), jnp.float32) * s, 'Wk': jax.random.normal(ks[2], (HID, H * DK), jnp.float32) * s, 'Wv': jax.random.normal(ks[3], (HID, H * DV), jnp.float32) * s, 'Ww': jax.random.normal(ks[4], (HID, H * M), jnp.float32) * s, 'cq': jax.random.normal(ks[5], (H * DK, KW), jnp.float32) * 0.2, 'ck': jax.random.normal(ks[6], (H * DK, KW), jnp.float32) * 0.2, 'cv': jax.random.normal(ks[7], (H * DV, KW), jnp.float32) * 0.2, 'Wf1': jax.random.normal(ks[8], (HID, DV), jnp.float32) * s, 'Wf2': jax.random.normal(ks[9], (DV, H * M), jnp.float32) * s, 'Wb': jax.random.normal(ks[10], (HID, H), jnp.float32) * s, 'Wg1': jax.random.normal(ks[11], (HID, DV), jnp.float32) * s, 'Wg2': jax.random.normal(ks[12], (DV, H * DV), jnp.float32) * s, 'bg2': jnp.zeros((H * DV,), jnp.float32), 'norm_w': jnp.ones((DV,), jnp.float32), 'Wo': jax.random.normal(ks[13], (H * DV, HID), jnp.float32) * s}
    _L0_attn_in = _L0_attn_setup()

    def _L0_ffn_setup():
        import jax, jax.numpy as jnp
        import numpy as np
        EPS = 1e-08

        def _quantize(w):
            gamma = jnp.mean(jnp.abs(w))
            return jnp.clip(jnp.round(w / (gamma + EPS)), -1.0, 1.0)

        def _bitlinear(x, w):
            return jnp.matmul(x, _quantize(w).T)
        key = jax.random.key(seed)
        k1, k2, k3, k4 = jax.random.split(key, 4)
        d, h = (512, 1408)
        x = jax.random.normal(k1, (4, 512, d), dtype=jnp.float32)
        w1 = jax.random.normal(k2, (h, d), dtype=jnp.float32)
        w2 = jax.random.normal(k3, (h, d), dtype=jnp.float32)
        w3 = jax.random.normal(k4, (d, h), dtype=jnp.float32)
        return {'x': x, 'w1': w1, 'w2': w2, 'w3': w3}
    _L0_ffn_in = _L0_ffn_setup()
    _d = {'L0_attn_hidden_states': _L0_attn_in['hidden_states'], 'L0_attn_Wq': _L0_attn_in['Wq'], 'L0_attn_Wk': _L0_attn_in['Wk'], 'L0_attn_Wv': _L0_attn_in['Wv'], 'L0_attn_Ww': _L0_attn_in['Ww'], 'L0_attn_cq': _L0_attn_in['cq'], 'L0_attn_ck': _L0_attn_in['ck'], 'L0_attn_cv': _L0_attn_in['cv'], 'L0_attn_Wf1': _L0_attn_in['Wf1'], 'L0_attn_Wf2': _L0_attn_in['Wf2'], 'L0_attn_Wb': _L0_attn_in['Wb'], 'L0_attn_Wg1': _L0_attn_in['Wg1'], 'L0_attn_Wg2': _L0_attn_in['Wg2'], 'L0_attn_bg2': _L0_attn_in['bg2'], 'L0_attn_norm_w': _L0_attn_in['norm_w'], 'L0_attn_Wo': _L0_attn_in['Wo'], 'L0_ffn_w1': _L0_ffn_in['w1'], 'L0_ffn_w2': _L0_ffn_in['w2'], 'L0_ffn_w3': _L0_ffn_in['w3']}
    _x0 = _d['L0_attn_hidden_states']
    _d['L0_attn_hidden_states'] = jax.random.normal(jax.random.fold_in(jax.random.key(seed), 1), (4, 512, 512), dtype=_x0.dtype)
    del _x0
    return _d

def reference(L0_attn_hidden_states, L0_attn_Wq, L0_attn_Wk, L0_attn_Wv, L0_attn_Ww, L0_attn_cq, L0_attn_ck, L0_attn_cv, L0_attn_Wf1, L0_attn_Wf2, L0_attn_Wb, L0_attn_Wg1, L0_attn_Wg2, L0_attn_bg2, L0_attn_norm_w, L0_attn_Wo, L0_ffn_w1, L0_ffn_w2, L0_ffn_w3):

    def _L0_attn_ref(hidden_states, Wq, Wk, Wv, Ww, cq, ck, cv, Wf1, Wf2, Wb, Wg1, Wg2, bg2, norm_w, Wo):
        import jax, jax.numpy as jnp
        import numpy as np
        B, T, HID = (1, 256, 512)
        H, DK, DV, M, KW = (16, 128, 128, 128, 4)
        SCALE = DK ** (-0.5)
        EPS = 1e-05

        def short_conv(x, w):
            K = w.shape[1]
            xp = jnp.pad(x, ((0, 0), (K - 1, 0), (0, 0)))
            t = x.shape[1]
            y = sum((xp[:, i:i + t] * w[:, i] for i in range(K)))
            return jax.nn.silu(y)

        def l2norm(x):
            return x * jax.lax.rsqrt(jnp.sum(x * x, axis=-1, keepdims=True) + 1e-06)

        def gsa2_scan(q, k, v, w, g, beta):
            b = q.shape[0]
            tm = lambda x: jnp.moveaxis(x, 1, 0)
            Sk0 = jnp.zeros((b, H, DK, M), q.dtype)
            Sv0 = jnp.zeros((b, H, M, DV), q.dtype)

            def step(carry, xs):
                Sk, Sv = carry
                q_t, k_t, v_t, w_t, g_t, b_t = xs
                gt = jnp.exp(g_t)
                bw = b_t[:, :, None] * w_t
                Sk = Sk * gt[:, :, None, :] + k_t[..., :, None] * bw[:, :, None, :]
                Sv = Sv * gt[..., None] + bw[..., None] * v_t[:, :, None, :]
                s = jnp.einsum('bhd,bhdm->bhm', q_t, Sk) * SCALE
                a = jax.nn.softmax(s, axis=-1)
                o_t = jnp.einsum('bhm,bhmd->bhd', a, Sv)
                return ((Sk, Sv), o_t)
            (_, _), o = jax.lax.scan(step, (Sk0, Sv0), (tm(q), tm(k), tm(v), tm(w), tm(g), tm(beta)))
            return jnp.moveaxis(o, 0, 1)
        h = hidden_states
        q = short_conv(h @ Wq, cq)
        k = short_conv(h @ Wk, ck)
        v = short_conv(h @ Wv, cv)
        w = short_conv(h @ Ww, cv)
        g = jax.nn.log_sigmoid(h @ Wf1 @ Wf2)
        beta = jax.nn.sigmoid(h @ Wb)
        rs = lambda x, d: x.reshape(x.shape[0], x.shape[1], -1, d)
        q, k = (rs(q, DK), rs(k, DK))
        v = rs(v, DV)
        w = l2norm(rs(w, M))
        g = rs(g, M)
        o = gsa2_scan(q, k, v, w, g, beta)
        gate = rs(h @ Wg1 @ Wg2 + bg2, DV)
        o = o * jax.lax.rsqrt(jnp.mean(o * o, axis=-1, keepdims=True) + EPS)
        o = o * norm_w * jax.nn.sigmoid(gate)
        o = o.reshape(o.shape[0], o.shape[1], -1)
        return o @ Wo

    def _L0_ffn_ref(x, w1, w2, w3):
        import jax, jax.numpy as jnp
        import numpy as np
        EPS = 1e-08

        def _quantize(w):
            gamma = jnp.mean(jnp.abs(w))
            return jnp.clip(jnp.round(w / (gamma + EPS)), -1.0, 1.0)

        def _bitlinear(x, w):
            return jnp.matmul(x, _quantize(w).T)
        x1 = _bitlinear(x, w1)
        x2 = _bitlinear(x, w2)
        hidden = jax.nn.sigmoid(x1) * x2
        return _bitlinear(hidden, w3)
    x = L0_attn_hidden_states
    x = x + 0.5 * _L0_ffn_ref(_layernorm(x, axis=-1), L0_ffn_w1, L0_ffn_w2, L0_ffn_w3)
    x = x + _L0_attn_ref(_layernorm(x, axis=-1), L0_attn_Wq, L0_attn_Wk, L0_attn_Wv, L0_attn_Ww, L0_attn_cq, L0_attn_ck, L0_attn_cv, L0_attn_Wf1, L0_attn_Wf2, L0_attn_Wb, L0_attn_Wg1, L0_attn_Wg2, L0_attn_bg2, L0_attn_norm_w, L0_attn_Wo)
    x = x + 0.5 * _L0_ffn_ref(_layernorm(x, axis=-1), L0_ffn_w1, L0_ffn_w2, L0_ffn_w3)
    return x

_drawn_inputs = setup_inputs


def setup_inputs(seed=0):
    import zlib

    import numpy as np

    out = dict(_drawn_inputs(seed))
    spreads = {'L0_attn_bg2': (0.0, 2.0), 'L0_attn_norm_w': (1.0, 0.6)}
    factors = {'L0_attn_Wq': 37.504,
     'L0_attn_Wk': 33.967,
     'L0_attn_Wv': 8.0,
     'L0_attn_Ww': 23.684,
     'L0_attn_cq': 37.628,
     'L0_attn_ck': 34.636,
     'L0_attn_cv': 8.0,
     'L0_attn_Wf1': 23.833,
     'L0_attn_Wf2': 23.8,
     'L0_attn_Wb': 8.0,
     'L0_attn_Wg1': 8.0,
     'L0_attn_Wg2': 8.0,
     'L0_attn_Wo': 8.0}
    for name, (base, spread) in spreads.items():
        noise = np.random.default_rng([zlib.crc32(name.encode()), seed]).standard_normal(out[name].shape)
        drawn = base * np.exp(spread * noise) if base else spread * noise
        out[name] = jnp.asarray(drawn.astype(out[name].dtype))
    for name, factor in factors.items():
        out[name] = (out[name] * factor).astype(out[name].dtype)
    return out
```

```python
from contextlib import ExitStack

import concourse.bass as bass
from concourse import mybir
from concourse.alu_op_type import AluOpType as ALU

FP32 = mybir.dt.float32
F32R = mybir.dt.float32r
INT32 = mybir.dt.int32
ACT = mybir.ActivationFunctionType
AX = mybir.AxisListType

P = 128
NB, T, HID = 4, 512, 512
NH = 16
FF = 1408
C = T // P
KT = HID // P
MT = FF // P
KW = 4
LEVELS = [1, 2, 4, 8, 16, 32, 64]
SCALE = P ** -0.5
LN_EPS = 1e-5
L2_EPS = 1e-6
RMS_EPS = 1e-5
Q_EPS = 1e-8


def halves(ap, level):
    return ap.rearrange("p (n two l) -> p n two l", two=2, l=level)


def packed(ap, level):
    return ap.rearrange("p (n l) -> p n l", l=level)


def ffn_phase(nc, first, x_in, x_out, w_t, wq_dram):
    with ExitStack() as ctx:
        def sb(name, shape, dt=FP32):
            return ctx.enter_context(nc.sbuf_tensor(f"{name}_{int(first)}", shape, dt))

        def sem(name):
            return ctx.enter_context(nc.semaphore(f"{name}_{int(first)}"))

        wq = [sb(f"wq{i}", [P, KT * FF], F32R) for i in range(3)]
        up = [wq[i][:, :].rearrange("p (k n) -> p k n", k=KT) for i in range(2)]
        down = wq[2][:, :].rearrange("p (m n) -> p m n", m=MT)
        x_sb = sb("x_sb", [P, NB * C, HID])
        x_new = sb("x_new", [P, C, HID])
        xn = sb("xn", [P, C, HID])
        stats = sb("stats", [P, C, 6])
        mv = sb("mv", [P, C, 2])
        gate = sb("gate", [P, 1])
        rstd = sb("rstd", [P, C])
        ve = sb("ve", [P, C])
        eps_t = sb("eps_t", [P, C])
        mhalf = sb("mhalf", [P, C])
        ident = sb("ident", [P, P])
        ones = sb("ones", [P, P])
        h_hi = sb("h_hi", [P, KT, T], F32R)
        h_lo = sb("h_lo", [P, KT, T], F32R)
        sig = sb("sig", [P, 2, T])
        hid = sb("hid", [P, 2, T])
        g_hi = [sb(f"g_hi{i}", [P, T], F32R) for i in range(2)]
        g_lo = [sb(f"g_lo{i}", [P, T], F32R) for i in range(2)]
        if first:
            raw = [sb(f"raw{i}", [P, KT * FF]) for i in range(2)]
            below = sb("below", [P, FF])
            junk = sb("junk", [P, FF])
            asum = sb("asum", [P, 3, KT])
            tot = sb("tot", [P, 3])
            gamma = sb("gamma", [P, 3])
            thr = sb("thr", [P, 3])
            nthr = sb("nthr", [P, 3])
        up_ps = [[ctx.enter_context(nc.psum_tensor(f"up_ps{i}{j}_{int(first)}", [P, T], FP32)) for j in range(2)]
                 for i in range(2)]
        out_ps = [ctx.enter_context(nc.psum_tensor(f"out_ps{c}_{int(first)}", [P, HID], FP32)) for c in range(C)]

        consts_ready = sem("consts_ready")
        raw_full = [sem(f"raw_full{i}") for i in range(3)]
        abs_summed = sem("abs_summed")
        total_ready = sem("total_ready")
        thr_step = sem("thr_step")
        below_ready = sem("below_ready")
        quantised = sem("quantised")
        wq_saved = sem("wq_saved")
        wq_full = [sem(f"wq_full{i}") for i in range(3)]
        x_full = [sem(f"x_full{b}") for b in range(NB)]
        stats_step = sem("stats_step")
        rstd_step = sem("rstd_step")
        xn_ready = sem("xn_ready")
        ln_transposed = sem("ln_transposed")
        h_split = sem("h_split")
        gate_in = sem("gate_in")
        value_in = sem("value_in")
        sig_ready = sem("sig_ready")
        hid_step = sem("hid_step")
        down_done = sem("down_done")
        out_added = sem("out_added")
        out_stored = sem("out_stored")
        block = ctx.enter_context(nc.Block())

        @block.sync
        def _(sp):
            def rows(dram, b):
                return dram[b * T:(b + 1) * T, :].rearrange("(c p) d -> p c d", p=P)

            sp.sem_inc(out_stored, 16)
            sp.dma_start(x_sb[:, 0:C, :], rows(x_in, 0)).then_inc(x_full[0], 16)
            for i in range(2):
                if first:
                    sp.dma_start(raw[i][:, :].rearrange("p (k n) -> p k n", k=KT),
                                 w_t[i].rearrange("(k p) n -> p k n", p=P)).then_inc(raw_full[i], 16)
                else:
                    sp.dma_start(wq[i][:, :].bitcast(FP32), wq_dram[i, :, :]).then_inc(wq_full[i], 16)
            for b in range(1, NB):
                sp.dma_start(x_sb[:, b * C:(b + 1) * C, :], rows(x_in, b)).then_inc(x_full[b], 16)
            if first:
                sp.wait_ge(quantised, KT)
                sp.dma_start(raw[0][:, :].rearrange("p (m n) -> p m n", m=MT),
                             w_t[2].rearrange("(m p) n -> p m n", p=P)).then_inc(raw_full[2], 16)
                for i in range(3):
                    sp.wait_ge(quantised, KT * (i + 1))
                    sp.dma_start(wq_dram[i, :, :], wq[i][:, :].bitcast(FP32)).then_inc(wq_saved, 16)
            else:
                sp.dma_start(wq[2][:, :].bitcast(FP32), wq_dram[2, :, :]).then_inc(wq_full[2], 16)
            with sp.Fori(0, NB) as b:
                sp.wait_ge(out_added, C * b + 2 * C)
                sp.dma_start(x_out[bass.ds(b * T, T), :].rearrange("(c p) d -> p c d", p=P),
                             x_new[:, :, :]).then_inc(out_stored, 16)
            sp.wait_ge(out_stored, 16 * NB + 16)
            if first:
                sp.wait_ge(wq_saved, 48)

        @block.gpsimd
        def _(pool):
            nc.gpsimd.memset(ident[:, :], 0.0).then_inc(consts_ready, 1)
            nc.gpsimd.memset(ones[:, :], 1.0).then_inc(consts_ready, 1)
            nc.gpsimd.memset(eps_t[:, :], LN_EPS).then_inc(consts_ready, 1)
            nc.gpsimd.memset(mhalf[:, :], -0.5).then_inc(consts_ready, 1)
            pool.wait_ge(consts_ready, 4)
            nc.gpsimd.affine_select(out=ident[:, :], in_=ident[:, :], compare_op=ALU.not_equal, fill=1.0, base=0,
                                    pattern=[[-1, P]], channel_multiplier=1).then_inc(consts_ready, 1)

            def deviation(i):
                pool.wait_ge(stats_step, 8 * i + 8)
                nc.gpsimd.tensor_tensor(ve[:, :], mv[:, :, 1], eps_t[:, :], ALU.add).then_inc(rstd_step, 1)
                pool.wait_ge(rstd_step, 2 * i + 1)
                nc.gpsimd.tensor_tensor(rstd[:, :], ve[:, :], mhalf[:, :], ALU.pow).then_inc(rstd_step, 1)

            deviation(0)
            with pool.Fori(1, NB) as i:
                deviation(i)

        @block.scalar
        def _(act):
            if first:
                for i in range(3):
                    act.wait_ge(raw_full[i], 16)
                    for k in range(KT):
                        nc.scalar.activation(junk[:, :], raw[i % 2][:, k * FF:(k + 1) * FF], ACT.Abs,
                                             accum_out=asum[:, i, k:k + 1]).then_inc(abs_summed, 1)
                        act.wait_ge(abs_summed, KT * i + k + 1)
            with act.Fori(0, NB) as b:
                for m in range(MT):
                    act.wait_ge(gate_in, MT * b + m + 1)
                    if m >= 2:
                        act.wait_ge(hid_step, 3 * (MT * b + m - 2 + MT) + 1)
                    nc.scalar.activation(sig[:, m % 2, :], up_ps[0][m % 2][:, :],
                                         ACT.Sigmoid).then_inc(sig_ready, 1)

        @block.vector
        def _(dve):
            def norm_stats(i):
                for c in range(C):
                    nc.vector.bn_stats(stats[:, c, :], x_rows(i, c)).then_inc(stats_step, 1)
                dve.wait_ge(stats_step, 8 * i + C)
                nc.vector.memset(gate[:, :], 0.0)
                for c in range(C):
                    nc.vector.bn_aggr(mv[:, c, :], stats[:, c, :]).then_inc(stats_step, 1)

            def x_rows(i, c):
                if isinstance(i, int):
                    return x_sb[:, i * C + c, :]
                return x_sb[:, bass.ds(i * C + c, 1), :].rearrange("p o d -> p (o d)")

            def norm_apply(i):
                dve.wait_ge(rstd_step, 2 * i + 2)
                if not isinstance(i, int):
                    dve.wait_ge(ln_transposed, KT * i)
                for c in range(C):
                    nc.vector.tensor_scalar(xn[:, c, :], x_rows(i, c), mv[:, c, 0:1], rstd[:, c:c + 1],
                                            ALU.subtract, ALU.mult).then_inc(xn_ready, 1)

            dve.sem_inc(hid_step, 3 * MT)
            dve.sem_inc(out_added, C)
            dve.wait_ge(x_full[0], 16)
            norm_stats(0)
            norm_apply(0)
            if first:
                for i in range(3):
                    s = 4 * i
                    dve.wait_ge(total_ready, i + 1)
                    nc.vector.tensor_reduce(tot[:, i:i + 1], out_ps[i][:, 0:KT], AX.X, ALU.add).then_inc(thr_step, 1)
                    dve.wait_ge(thr_step, s + 1)
                    nc.vector.tensor_scalar(gamma[:, i:i + 1], tot[:, i:i + 1], 1.0 / (FF * HID), Q_EPS,
                                            ALU.mult, ALU.add).then_inc(thr_step, 1)
                    dve.wait_ge(thr_step, s + 2)
                    nc.vector.tensor_scalar(nthr[:, i:i + 1], gamma[:, i:i + 1], -0.5, None,
                                            ALU.mult).then_inc(thr_step, 1)
                    nc.vector.tensor_scalar(thr[:, i:i + 1], gamma[:, i:i + 1], 0.5, None,
                                            ALU.mult).then_inc(thr_step, 1)
                    dve.wait_ge(thr_step, s + 4)
                    for k in range(KT):
                        piece = slice(k * FF, (k + 1) * FF)
                        dve.wait_ge(quantised, KT * i + k)
                        nc.vector.tensor_scalar(below[:, :], raw[i % 2][:, piece], nthr[:, i:i + 1], None,
                                                ALU.is_lt).then_inc(below_ready, 1)
                        dve.wait_ge(below_ready, KT * i + k + 1)
                        nc.vector.scalar_tensor_tensor(wq[i][:, piece], raw[i % 2][:, piece], thr[:, i:i + 1],
                                                       below[:, :], ALU.is_gt, ALU.subtract).then_inc(quantised, 1)

            def split_norm(b):
                for k in range(KT):
                    bank = up_ps[k // 2][k % 2]
                    dve.wait_ge(ln_transposed, KT * b + k + 1)
                    nc.vector.tensor_copy(h_hi[:, k, :], bank[:, :]).then_inc(h_split, 1)
                    dve.wait_ge(h_split, 2 * (KT * b + k) + 1)
                    nc.vector.tensor_tensor(h_lo[:, k, :], bank[:, :], h_hi[:, k, :].bitcast(FP32),
                                            ALU.subtract).then_inc(h_split, 1)

            def batch(b, last):
                split_norm(b)
                for m in range(MT):
                    n = MT * b + m
                    dve.wait_ge(sig_ready, n + 1)
                    dve.wait_ge(value_in, n + 1)
                    nc.vector.tensor_tensor(hid[:, m % 2, :], up_ps[1][m % 2][:, :], sig[:, m % 2, :],
                                            ALU.mult).then_inc(hid_step, 1)
                    dve.wait_ge(hid_step, 3 * (n + MT) + 1)
                    if m >= 2:
                        dve.wait_ge(down_done, n - 1)
                    nc.vector.tensor_copy(g_hi[m % 2][:, :], hid[:, m % 2, :]).then_inc(hid_step, 1)
                    dve.wait_ge(hid_step, 3 * (n + MT) + 2)
                    nc.vector.tensor_tensor(g_lo[m % 2][:, :], hid[:, m % 2, :], g_hi[m % 2][:, :].bitcast(FP32),
                                            ALU.subtract).then_inc(hid_step, 1)
                    if m == 3 and not last:
                        norm_stats(b + 1)
                    if m == 5 and not last:
                        norm_apply(b + 1)
                dve.wait_ge(down_done, MT * b + MT)
                dve.wait_ge(out_stored, 16 * b + 16)
                for c in range(C):
                    nc.vector.scalar_tensor_tensor(x_new[:, c, :], out_ps[c][:, :], 0.5, x_rows(b, c),
                                                   ALU.mult, ALU.add).then_inc(out_added, 1)

            for b in range(1, NB):
                dve.wait_ge(x_full[b], 16)
            with dve.Fori(0, NB - 1) as b:
                batch(b, False)
            batch(NB - 1, True)

        @block.tensor
        def _(pe):
            pe.wait_ge(consts_ready, 5)
            if first:
                for i in range(3):
                    pe.wait_ge(abs_summed, KT * (i + 1))
                    nc.tensor.matmul(out_ps[i][:, 0:KT], ones[:, :], asum[:, i, :], start=True,
                                     stop=True).then_inc(total_ready, 1)
                pe.wait_ge(quantised, 3 * KT)
            else:
                for i in range(3):
                    pe.wait_ge(wq_full[i], 16)

            def down_tile(b, m):
                pe.wait_ge(hid_step, 3 * (MT * b + m + MT) + 3)
                if m == 0:
                    pe.wait_ge(out_added, C * b + C)
                for c in range(C):
                    for part in (g_hi, g_lo):
                        last = nc.tensor.matmul(out_ps[c][:, :], part[m % 2][:, c * P:(c + 1) * P], down[:, m, :],
                                                start=(m == 0 and part is g_hi),
                                                stop=(m == MT - 1 and part is g_lo))
                last.then_inc(down_done, 1)

            with pe.Fori(0, NB) as b:
                pe.wait_ge(xn_ready, C * b + C)
                pe.wait_ge(hid_step, 3 * MT * b + 3 * MT)
                for k in range(KT):
                    for c in range(C):
                        last = nc.tensor.transpose(up_ps[k // 2][k % 2][:, c * P:(c + 1) * P],
                                                   xn[:, c, k * P:(k + 1) * P], ident[:, :])
                    last.then_inc(ln_transposed, 1)
                pe.wait_ge(h_split, 2 * KT * (b + 1))
                for m in range(MT):
                    if m >= 2:
                        pe.wait_ge(hid_step, 3 * (MT * b + m - 2 + MT) + 1)
                    for which, ready in ((0, gate_in), (1, value_in)):
                        for k in range(KT):
                            for part in (h_hi, h_lo):
                                last = nc.tensor.matmul(up_ps[which][m % 2][:, :],
                                                        up[which][:, k, m * P:(m + 1) * P], part[:, k, :],
                                                        start=(k == 0 and part is h_hi),
                                                        stop=(k == KT - 1 and part is h_lo))
                        last.then_inc(ready, 1)
                    if m >= 1:
                        down_tile(b, m - 1)
                down_tile(b, MT - 1)


PE_PROJ = "w k v g q".split()
PE_SCAN = ("kT gate wT x1T x2T x4T x8T vT A x16T x32T x64T xbT s0 s2 s4 s8 U0 U1 U2 s16 skT s32 sst s64 sT aT "
           "a2d a2_1 a2_2 a2_4 a2_8 a2_16 a2_32 a2_64 o onT").split()
ACT_PROJ = "acc_w acc_k acc_v w xb k g acc_q".split()
ACT_SCAN = "sg sq xt0 xt1 xt2 xt4 q v xt8 xt16 xt32 xt64 xtb s0 sk e0 e1 e2 e3 aT osq".split()
DVE_PROJ = ("tap cw1 cw2 cw3 ck1 ck2 ck3 cv1 cv2 cv3 f2 c2 f4 c4 f8 c8 f16 c16 f32 c32 f64 c64 f128 G").split()
DVE_SCAN = ("ss cq1 cq2 cq3 kr vr As am0 am1 am2 am4 am8 am16 "
            "am32 am64 m2 m4 m8 St0 St1 St2 m16 m32 mst m64 mx nms rs a2d a2_1 a2_2 a2_4 a2_8 a2_16 a2_32 a2_64 "
            "oss on og").split()
POOL_SCAN = ("x1 b1 x2 b2 x4 b4 x8 b8 x16 b16 x32 b32 x64 b64 bne bnp bn ad2 ad4 ad8 ad16 ad32 adst ad64 "
             "y2 y4 y8 y16 y32 y64 yst r1 r2 r3 r4 r5").split()
PE_EDGE = ["lnT0", "lnT1", "lnT2", "lnT3", "f1", "g1", "beta"] + [f"wo{h}" for h in range(NH)]
ACT_EDGE = "hT0 hT1 hT2 hT3 f1 g1 beta".split()
DVE_EDGE = "st0 st1 st2 st3 ag0 ag1 ag2 ag3 xn0 xn1 xn2 xn3 add0 add1 add2 add3".split()
POOL_EDGE = "ve rstd".split()


def after(steps, name, u):
    return u * len(steps) + (len(steps) + steps.index(name) + 1)


def before(steps, u):
    return u * len(steps) + len(steps)


def attention_phase(nc, x_in, x_out, a):
    with ExitStack() as ctx:
        def sb(name, shape, dt=FP32):
            return ctx.enter_context(nc.sbuf_tensor(name, shape, dt))

        def ps(name, width=T):
            return ctx.enter_context(nc.psum_tensor(name, [P, width], FP32))

        def sem(name):
            return ctx.enter_context(nc.semaphore(name))

        ident = sb("ident", [P, P])
        mask = {l: sb(f"mask{l}", [P, T // 2]) for l in LEVELS}
        l2_eps = sb("l2_eps", [P, C])
        rms_eps = sb("rms_eps", [P, C])
        ln_eps = sb("ln_eps", [P, C])
        mhalf = sb("mhalf_a", [P, C])
        hold = sb("hold", [P, 1])
        wf1 = sb("wf1", [P, KT, P])
        wg1 = sb("wg1", [P, KT, P])
        wb = sb("wb", [P, KT, NH])
        per_head = sb("per_head", [P, NH, 3 * KW + 1])
        norm_w = sb("norm_w", [P, 1])
        slot = {n: sb(f"slot_{n}", [P, HID]) for n in "wkvq"}
        slot["g"] = sb("slot_g", [P, P])
        slot["gate"] = sb("slot_gate", [P, P])
        wo = [sb(f"wo{i}", [P, HID]) for i in range(4)]
        xn = sb("xn_a", [P, C, HID])
        res = sb("res", [P, C, HID])
        stats = sb("stats_a", [P, C, 6])
        mv = sb("mv_a", [P, C, 2])
        ve = sb("ve_a", [P, C])
        rstd = sb("rstd_a", [P, C])
        hT = sb("hT", [P, KT, T])
        f1T = sb("f1T", [P, T])
        g1T = sb("g1T", [P, T])
        beta = sb("beta", [P, C, NH])
        og = sb("og", [P, NH, T])
        tap = sb("tap", [P, 3 * KW + 1])
        TAP = {"q": 0, "k": KW, "v": 2 * KW, "w": 2 * KW}
        BIAS = 3 * KW
        acc = {n: sb(f"acc_{n}", [P, T]) for n in "wkvq"}
        w, k, v, q, g, sg, xb = (sb(f"u_{n}", [P, T]) for n in "w k v q g sg xb".split())
        F = {l: sb(f"F{l}", [P, T]) for l in LEVELS[1:] + [P]}
        cc = {l: sb(f"cc{l}", [P, T // (2 * l), 2]) for l in LEVELS[1:]}
        G = sb("G", [P, T])
        XS = {l: sb(f"XS{l}", [P, T]) for l in LEVELS}
        XT = {l: sb(f"XT{l}", [P, C, P]) for l in [0] + LEVELS}
        XTB = sb("XTB", [P, C - 1, P])
        sq = sb("sq", [P, C, P])
        ss = sb("ss", [P, C])
        bn1, bn2, bn = (sb(n, [P, C]) for n in ("bn1", "bn2", "bn"))
        kv = sb("kv", [P, C, 2 * P])
        As = sb("As", [P, T])
        AM = {l: sb(f"AM{l}", [P, T // 2]) for l in LEVELS}
        AM[0] = sb("AM0", [P, T])
        tmp = [sb(f"tmp{i}", [P, T // 2]) for i in range(2)] + [sb("tmp2", [P, T - P])]
        state = sb("state", [P, C - 1, 2 * P])
        Sk = sb("Sk", [P, C - 1, P])
        s = sb("s", [P, T])
        nmx, nms, rsum, rs, oss = (sb(n, [P, C]) for n in "nmx nms rsum rs oss".split())
        r1, r2, r3, r4, r5 = (sb(n, [P, C]) for n in "r1 r2 r3 r4 r5".split())
        au = sb("au", [P, C, P])
        aT = sb("aT", [P, T])
        Y = {l: sb(f"Y{l}", [P, T // 2]) for l in LEVELS[1:]}
        Yst = sb("Yst", [P, T - P])
        A2 = sb("A2", [P, T])
        on = sb("on", [P, C, P])

        pr = [ps(f"pr{i}") for i in range(2)]
        tb = [ps(f"tb{i}") for i in range(2)]
        lv = [ps(f"lv{i}") for i in range(2)]
        mi = [ps(f"mi{i}") for i in range(2)]

        pe_proj, pe_scan, pe_edge = sem("pe_proj"), sem("pe_scan"), sem("pe_edge")
        act_proj, act_scan, act_edge = sem("act_proj"), sem("act_scan"), sem("act_edge")
        dve_proj, dve_scan, dve_edge = sem("dve_proj"), sem("dve_scan"), sem("dve_edge")
        pool_scan, pool_edge, pool_consts = sem("pool_scan"), sem("pool_edge"), sem("pool_consts")
        dve_consts = sem("dve_consts")
        small_full = sem("small_full")
        slot_full = {n: sem(f"slot_full_{n}") for n in slot}
        wo_full = [sem(f"wo_full{i}") for i in range(4)]
        xn_full, res_full, res_stored = sem("xn_full"), sem("res_full"), sem("res_stored")
        block = ctx.enter_context(nc.Block())
        SMALL = 5
        bank = {"wT": tb[0], "x1T": tb[1], "x2T": tb[0], "x4T": tb[1], "x8T": tb[0], "x16T": tb[1], "x32T": tb[0],
                "x64T": tb[1], "xbT": tb[0], "skT": tb[1], "sT": tb[0], "aT": tb[1], "onT": tb[0],
                "s0": lv[0], "s2": lv[1], "s4": lv[0], "s8": lv[1], "s16": lv[0], "s32": lv[1], "sst": lv[0],
                "s64": lv[1], "a2d": lv[0], "a2_1": lv[1], "a2_2": lv[0], "a2_4": lv[1], "a2_8": lv[0],
                "a2_16": lv[1], "a2_32": lv[0], "a2_64": lv[1],
                "kT": mi[0], "U0": mi[0], "U2": mi[0], "o": mi[0], "vT": mi[1], "A": mi[1], "U1": mi[1],
                "g": mi[1], "w": pr[0], "v": pr[0], "gate": pr[0], "k": pr[1], "q": pr[1]}

        def ck_(t, c, width=P):
            return t[:, c * width:(c + 1) * width]

        def chunks(t):
            return t[:, :].rearrange("p (c n) -> p c n", c=C)

        def rows(dram, b):
            r = dram[b * T:(b + 1) * T, :] if isinstance(b, int) else dram[bass.ds(b * T, T), :]
            return r.rearrange("(c p) d -> p c d", p=P)

        @block.sync
        def _(sp):
            def load_slots(n, u, h):
                src = {"w": a["ww"], "k": a["wk"], "g": a["wf2"], "v": a["wv"], "q": a["wq"], "gate": a["wg2"]}[n]
                src = src[h, :, :] if isinstance(h, int) else src[bass.ds(h, 1), :, :].rearrange("o p n -> (o p) n")
                if u is not None:
                    if n == "gate":
                        sp.wait_ge(pe_scan, after(PE_SCAN, "gate", u))
                    else:
                        sp.wait_ge(pe_proj, after(PE_PROJ, n, u))
                sp.dma_start(slot[n][:, :], src).then_inc(slot_full[n], 16)

            sp.dma_start(xn[:, :, :], rows(x_in, 0)).then_inc(xn_full, 16)
            for dst, src in ((wf1, a["wf1"]), (wg1, a["wg1"]), (wb, a["wb"])):
                sp.dma_start(dst[:, :, :], src.rearrange("(k p) n -> p k n", p=P)).then_inc(small_full, 16)
            sp.dma_start(per_head[:, :, :], a["per_head"]).then_inc(small_full, 16)
            sp.dma_start(norm_w[:, :], a["norm_w"]).then_inc(small_full, 16)
            sp.dma_start(res[:, :, :], rows(x_in, 0)).then_inc(res_full, 16)
            for n in ("w", "k", "v", "g", "q", "gate"):
                load_slots(n, None, 0)

            def batch(b, final):
                with sp.Fori(0, NH - 1) as h:
                    for n in ("w", "k", "v", "g", "q", "gate"):
                        load_slots(n, b * NH + h, h + 1)
                if not final:
                    for n in ("w", "k", "v", "g", "q"):
                        load_slots(n, b * NH + (NH - 1), 0)
                    sp.wait_ge(pe_edge, after(PE_EDGE, "lnT3", b))
                    sp.dma_start(xn[:, :, :], rows(x_in, b + 1)).then_inc(xn_full, 16)
                for h in range(NH):
                    if h >= 4:
                        sp.wait_ge(pe_edge, after(PE_EDGE, f"wo{h - 4}", b))
                    else:
                        sp.wait_ge(pe_edge, after(PE_EDGE, "beta", b))
                    sp.dma_start(wo[h % 4][:, :], a["wo"][h, :, :]).then_inc(wo_full[h % 4], 16)
                if not final:
                    load_slots("gate", b * NH + (NH - 1), 0)
                sp.wait_ge(dve_edge, after(DVE_EDGE, "add3", b))
                sp.dma_start(rows(x_out, b), res[:, :, :]).then_inc(res_stored, 16)
                if not final:
                    sp.wait_ge(res_stored, (b + 1) * 16)
                    sp.dma_start(res[:, :, :], rows(x_in, b + 1)).then_inc(res_full, 16)

            with sp.Fori(0, NB - 1) as b:
                batch(b, False)
            batch(NB - 1, True)
            sp.wait_ge(res_stored, 16 * NB)

        @block.gpsimd
        def _(pool):
            for steps, done in ((POOL_SCAN, pool_scan), (POOL_EDGE, pool_edge)):
                pool.sem_inc(done, len(steps))
            nc.gpsimd.memset(ident[:, :], 0.0).then_inc(pool_consts, 1)
            nc.gpsimd.memset(l2_eps[:, :], L2_EPS).then_inc(pool_consts, 1)
            nc.gpsimd.memset(rms_eps[:, :], RMS_EPS).then_inc(pool_consts, 1)
            nc.gpsimd.memset(ln_eps[:, :], LN_EPS).then_inc(pool_consts, 1)
            nc.gpsimd.memset(mhalf[:, :], -0.5).then_inc(pool_consts, 1)
            for l in LEVELS:
                nc.gpsimd.memset(mask[l][:, :], 1.0).then_inc(pool_consts, 1)
            pool.wait_ge(pool_consts, 12)
            nc.gpsimd.affine_select(out=ident[:, :], in_=ident[:, :], compare_op=ALU.not_equal, fill=1.0, base=0,
                                    pattern=[[-1, P]], channel_multiplier=1).then_inc(pool_consts, 1)
            for i, l in enumerate(LEVELS):
                m4 = mask[l][:, :].rearrange("p (c n l) -> p c n l", c=C, l=l)
                blocks = P // (2 * l)
                nc.gpsimd.affine_select(out=m4, in_=m4, compare_op=ALU.is_ge, fill=0.0, base=0,
                                        pattern=[[0, C], [-2 * l, blocks], [0, l]],
                                        channel_multiplier=1).then_inc(pool_consts, 1)
                pool.wait_ge(pool_consts, 14 + 2 * i)
                nc.gpsimd.affine_select(out=m4, in_=m4, compare_op=ALU.is_ge, fill=0.0, base=l - 1,
                                        pattern=[[0, C], [2 * l, blocks], [0, l]],
                                        channel_multiplier=-1).then_inc(pool_consts, 1)
            pool.wait_ge(pool_consts, 27)
            pool.wait_ge(small_full, 16 * SMALL)
            pool.wait_ge(dve_consts, 14)

            def tt(out, in0, in1, op=ALU.mult, done=pool_scan):
                return nc.gpsimd.tensor_tensor(out, in0, in1, op)

            def scan(u, h):
                def own(name):
                    pool.wait_ge(pool_scan, after(POOL_SCAN, name, u))

                gh = {l: halves(g[:, :], l) for l in LEVELS}

                def decay_to_target(l):
                    return gh[l][:, :, 1, 0:1].to_broadcast([P, T // (2 * l), l])

                pool.wait_ge(act_proj, after(ACT_PROJ, "g", u))
                pool.wait_ge(pe_scan, u * len(PE_SCAN) + PE_SCAN.index("a2_64") + 1)
                prev = None
                for l in LEVELS:
                    if l == 1:
                        src = halves(w[:, :], 1)[:, :, 0, :]
                    else:
                        src = halves(xb[:, :], l)[:, :, 0, :]
                        own(prev)
                    tt(halves(XS[l][:, :], l)[:, :, 0, :], src, decay_to_target(l)).then_inc(pool_scan, 1)
                    if l == 1:
                        tt(halves(xb[:, :], 1)[:, :, 0, :], src, decay_to_target(1)).then_inc(pool_scan, 1)
                    else:
                        own(f"x{l}")
                        pool.wait_ge(dve_proj, after(DVE_PROJ, f"f{l}", u))
                        end = halves(F[l][:, :], l)[:, :, 1, l - 1:l].to_broadcast([P, T // (2 * l), l])
                        tt(halves(xb[:, :], l)[:, :, 0, :], halves(XS[l][:, :], l)[:, :, 0, :],
                           end).then_inc(pool_scan, 1)
                    prev = f"b{l}"
                    if l == 64:
                        pool.wait_ge(dve_scan, after(DVE_SCAN, "ss", u))
                        tt(bn1[:, :], ss[:, :], l2_eps[:, :], ALU.add).then_inc(pool_scan, 1)
                        own("bne")
                        tt(bn2[:, :], bn1[:, :], mhalf[:, :], ALU.pow).then_inc(pool_scan, 1)
                        own("bnp")
                        b_h = beta[:, :, h] if isinstance(h, int) else \
                            beta[:, :, bass.ds(h, 1)].rearrange("p c o -> p (c o)")
                        tt(bn[:, :], bn2[:, :], b_h).then_inc(pool_scan, 1)
                pool.wait_ge(act_scan, after(ACT_SCAN, "s0", u))
                prev = None
                for i, l in enumerate(LEVELS[1:]):
                    if l == 64:
                        pool.wait_ge(dve_scan, after(DVE_SCAN, "mst", u))
                        own(prev)
                        tt(s[:, P:T], s[:, P:T], tmp[2][:, :], ALU.add).then_inc(pool_scan, 1)
                        prev = "adst"
                    pool.wait_ge(dve_scan, after(DVE_SCAN, f"m{l}", u))
                    if prev:
                        own(prev)
                    dst = halves(s[:, :], l)[:, :, 1, :]
                    tt(dst, dst, packed(tmp[i % 2][:, 0:T // 2], l), ALU.add).then_inc(pool_scan, 1)
                    prev = f"ad{l}"
                pool.wait_ge(act_scan, after(ACT_SCAN, "aT", u))
                for l in LEVELS[1:]:
                    tt(packed(Y[l][:, :], l), halves(aT[:, :], l)[:, :, 1, :],
                       halves(F[l][:, :], l)[:, :, 1, :]).then_inc(pool_scan, 1)
                tt(Yst[:, :], aT[:, P:T], G[:, P:T]).then_inc(pool_scan, 1)
                pool.wait_ge(dve_scan, after(DVE_SCAN, "rs", u))
                tt(r1[:, :], rs[:, :], rs[:, :]).then_inc(pool_scan, 1)
                own("r1")
                pool.wait_ge(dve_scan, after(DVE_SCAN, "oss", u))
                tt(r2[:, :], r1[:, :], oss[:, :]).then_inc(pool_scan, 1)
                own("r2")
                tt(r3[:, :], r2[:, :], rms_eps[:, :], ALU.add).then_inc(pool_scan, 1)
                own("r3")
                tt(r4[:, :], r3[:, :], mhalf[:, :], ALU.pow).then_inc(pool_scan, 1)
                own("r4")
                tt(r5[:, :], r4[:, :], rs[:, :]).then_inc(pool_scan, 1)

            with pool.Fori(0, NB) as b:
                pool.wait_ge(dve_edge, after(DVE_EDGE, "ag3", b))
                tt(ve[:, :], mv[:, :, 1], ln_eps[:, :], ALU.add).then_inc(pool_edge, 1)
                pool.wait_ge(pool_edge, after(POOL_EDGE, "ve", b))
                tt(rstd[:, :], ve[:, :], mhalf[:, :], ALU.pow).then_inc(pool_edge, 1)
                with pool.Fori(0, NH) as h:
                    scan(b * NH + h, h)

        @block.scalar
        def _(act):
            for steps, done in ((ACT_PROJ, act_proj), (ACT_SCAN, act_scan), (ACT_EDGE, act_edge)):
                act.sem_inc(done, len(steps))
            act.wait_ge(small_full, 16 * SMALL)

            def first_tap(n, unit):
                at = TAP[n] + KW - 1
                if n == "w":
                    act.wait_ge(dve_proj, after(DVE_PROJ, "tap", unit))
                act.wait_ge(pe_proj, after(PE_PROJ, n, unit))
                nc.scalar.activation(acc[n][:, :], bank[n][:, :], ACT.Copy,
                                     scale=tap[:, at:at + 1]).then_inc(act_proj, 1)

            def proj_slots(n, w_read):
                act.wait_ge(dve_proj, after(DVE_PROJ, "cw3", n))
                act.wait_ge(pe_scan, w_read)
                nc.scalar.activation(w[:, :], acc["w"][:, :], ACT.Silu).then_inc(act_proj, 1)
                nc.scalar.activation(xb[:, :], acc["w"][:, :], ACT.Silu).then_inc(act_proj, 1)
                act.wait_ge(dve_proj, after(DVE_PROJ, "ck3", n))
                nc.scalar.activation(k[:, :], acc["k"][:, :], ACT.Silu).then_inc(act_proj, 1)

            def proj_decay(n):
                act.wait_ge(pe_proj, after(PE_PROJ, "g", n))
                nc.scalar.activation(g[:, :], bank["g"][:, :], ACT.Sigmoid).then_inc(act_proj, 1)

            def scan(u, h, more):
                def pe_done(name):
                    act.wait_ge(pe_scan, after(PE_SCAN, name, u))

                def copy_out(dst, name):
                    pe_done(name)
                    nc.scalar.activation(dst, bank[name][:, :], ACT.Copy).then_inc(act_scan, 1)

                pe_done("gate")
                act.wait_ge(dve_scan, before(DVE_SCAN, u))
                nc.scalar.activation(sg[:, :], bank["gate"][:, :], ACT.Sigmoid,
                                     bias=tap[:, BIAS:BIAS + 1]).then_inc(act_scan, 1)
                pe_done("wT")
                nc.scalar.activation(sq[:, :, :], chunks(bank["wT"]), ACT.Square).then_inc(act_scan, 1)
                nc.scalar.activation(XT[0][:, :, :], chunks(bank["wT"]), ACT.Copy).then_inc(act_scan, 1)
                copy_out(XT[1][:, :, :].rearrange("p c n -> p (c n)"), "x1T")
                copy_out(XT[2][:, :, :].rearrange("p c n -> p (c n)"), "x2T")
                for l in LEVELS[2:]:
                    copy_out(XT[l][:, :, :].rearrange("p c n -> p (c n)"), f"x{l}T")
                    if l == 4:
                        act.wait_ge(dve_scan, after(DVE_SCAN, "cq3", u))
                        nc.scalar.activation(q[:, :], acc["q"][:, :], ACT.Silu).then_inc(act_scan, 1)
                        act.wait_ge(dve_proj, after(DVE_PROJ, "cv3", u))
                        nc.scalar.activation(v[:, :], acc["v"][:, :], ACT.Silu).then_inc(act_scan, 1)
                if more:
                    first_tap("w", u + 1)
                pe_done("xbT")
                nc.scalar.activation(XTB[:, :, :].rearrange("p c n -> p (c n)"), bank["xbT"][:, 0:T - P],
                                     ACT.Copy).then_inc(act_scan, 1)
                copy_out(s[:, :], "s0")
                pe_done("skT")
                nc.scalar.activation(Sk[:, :, :].rearrange("p c n -> p (c n)"), bank["skT"][:, 0:T - P],
                                     ACT.Copy).then_inc(act_scan, 1)
                act.wait_ge(dve_scan, after(DVE_SCAN, "nms", u))
                for c in range(C):
                    nc.scalar.activation(au[:, c, :], ck_(bank["sT"], c), ACT.Exp, scale=SCALE, bias=nms[:, c:c + 1],
                                         accum_out=rsum[:, c:c + 1]).then_inc(act_scan, 1)
                if more:
                    first_tap("k", u + 1)
                copy_out(aT[:, :], "aT")
                if more:
                    first_tap("v", u + 1)
                    proj_slots(u + 1, after(PE_SCAN, "a2d", u))
                pe_done("o")
                nc.scalar.activation(sq[:, :, :], chunks(bank["o"]), ACT.Square,
                                     scale=P ** -0.5).then_inc(act_scan, 1)
                if more:
                    proj_decay(u + 1)
                    first_tap("q", u + 1)

            with act.Fori(0, NB) as b:
                for kk in range(KT):
                    act.wait_ge(pe_edge, after(PE_EDGE, f"lnT{kk}", b))
                    nc.scalar.activation(hT[:, kk, :], (lv + tb)[kk][:, :], ACT.Copy).then_inc(act_edge, 1)
                act.wait_ge(pe_edge, after(PE_EDGE, "f1", b))
                nc.scalar.activation(f1T[:, :], mi[0][:, :], ACT.Copy).then_inc(act_edge, 1)
                act.wait_ge(pe_edge, after(PE_EDGE, "g1", b))
                nc.scalar.activation(g1T[:, :], mi[1][:, :], ACT.Copy).then_inc(act_edge, 1)
                act.wait_ge(pe_edge, after(PE_EDGE, "beta", b))
                nc.scalar.activation(beta[:, :, :].rearrange("p c h -> p (c h)"), pr[0][:, 0:C * NH],
                                     ACT.Sigmoid).then_inc(act_edge, 1)
                n = b * NH
                first_tap("w", n)
                first_tap("k", n)
                first_tap("v", n)
                proj_slots(n, before(PE_SCAN, n))
                proj_decay(n)
                first_tap("q", n)
                with act.Fori(0, NH - 1) as h:
                    scan(b * NH + h, h, True)
                scan(b * NH + (NH - 1), NH - 1, False)

        @block.vector
        def _(dve):
            for steps, done in ((DVE_PROJ, dve_proj), (DVE_SCAN, dve_scan), (DVE_EDGE, dve_edge)):
                dve.sem_inc(done, len(steps))
            for l in LEVELS:
                nc.vector.memset(XS[l][:, :], 0.0).then_inc(dve_consts, 1)
            nc.vector.memset(F[2][:, :], 1.0).then_inc(dve_consts, 1)
            for l in LEVELS[1:]:
                nc.vector.memset(cc[l][:, :, :], 1.0).then_inc(dve_consts, 1)
            dve.wait_ge(dve_consts, 14)
            dve.wait_ge(pool_consts, 27)
            dve.wait_ge(small_full, 16 * SMALL)

            def taps(n, unit, sem_, table):
                dve.wait_ge(act_proj, after(ACT_PROJ, f"acc_{n}", unit))
                for j in range(1, KW):
                    if j > 1:
                        dve.wait_ge(sem_, after(table, f"c{n}{j - 1}", unit))
                    at = TAP[n] + KW - 1 - j
                    nc.vector.scalar_tensor_tensor(acc[n][:, j:], bank[n][:, 0:T - j], tap[:, at:at + 1],
                                                   acc[n][:, j:], ALU.mult, ALU.add).then_inc(sem_, 1)

            def head_taps(n, h):
                src = per_head[:, h, :] if isinstance(h, int) else \
                    per_head[:, bass.ds(h, 1), :].rearrange("p o n -> p (o n)")
                nc.vector.tensor_scalar(tap[:, :], src, 1.0, None, ALU.mult).then_inc(dve_proj, 1)

            def f_step(n, name):
                if name == "f2":
                    dve.wait_ge(act_proj, after(ACT_PROJ, "g", n))
                    nc.vector.tensor_copy(halves(F[2][:, :], 1)[:, :, 1, :],
                                          halves(g[:, :], 1)[:, :, 1, :]).then_inc(dve_proj, 1)
                elif name == "G":
                    dve.wait_ge(dve_proj, after(DVE_PROJ, "f128", n))
                    nc.vector.tensor_tensor(chunks(G), chunks(F[P]), chunks(g)[:, :, 0:1].to_broadcast([P, C, P]),
                                            ALU.mult).then_inc(dve_proj, 1)
                elif name[0] == "c":
                    l = int(name[1:])
                    dve.wait_ge(dve_proj, after(DVE_PROJ, f"f{l}", n))
                    nc.vector.tensor_tensor(cc[l][:, :, 1:2], halves(F[l][:, :], l)[:, :, 0, l - 1:l],
                                            halves(g[:, :], l)[:, :, 1, 0:1], ALU.mult).then_inc(dve_proj, 1)
                else:
                    l = int(name[1:]) // 2
                    dve.wait_ge(dve_proj, after(DVE_PROJ, f"c{l}", n))
                    whole = cc[l][:, :, :].rearrange("p n (two o) -> p (n two) o", o=1)
                    nc.vector.tensor_tensor(packed(F[2 * l][:, :], l), packed(F[l][:, :], l),
                                            whole.to_broadcast([P, T // l, l]), ALU.mult).then_inc(dve_proj, 1)

            F_STEPS = DVE_PROJ[DVE_PROJ.index("f2"):]

            def scan(u, h, more):
                def own(name):
                    dve.wait_ge(dve_scan, after(DVE_SCAN, name, u))

                def pe_done(name):
                    dve.wait_ge(pe_scan, after(PE_SCAN, name, u))

                def tt(out, in0, in1, op=ALU.mult):
                    return nc.vector.tensor_tensor(out, in0, in1, op)

                dve.wait_ge(act_scan, after(ACT_SCAN, "sq", u))
                nc.vector.tensor_reduce(ss[:, :], sq[:, :, :], AX.X, ALU.add).then_inc(dve_scan, 1)
                taps("q", u, dve_scan, DVE_SCAN)
                if more:
                    own("cq3")
                    head_taps(u + 1, h + 1)
                dve.wait_ge(pool_scan, after(POOL_SCAN, "bn", u))
                by_step = bn[:, :].rearrange("p (c o) -> p c o", o=1).to_broadcast([P, C, P])
                tt(kv[:, :, 0:P], chunks(bank["kT"]), by_step).then_inc(dve_scan, 1)
                pe_done("vT")
                tt(kv[:, :, P:2 * P], chunks(bank["vT"]), by_step).then_inc(dve_scan, 1)
                pe_done("A")
                tt(chunks(As), chunks(bank["A"]), by_step).then_inc(dve_scan, 1)
                own("As")
                eye = ident[:, :].rearrange("p (o n) -> p o n", o=1).to_broadcast([P, C, P])
                tt(chunks(AM[0]), chunks(As), eye).then_inc(dve_scan, 1)
                for l in LEVELS:
                    tt(packed(AM[l][:, :], l), halves(As[:, :], l)[:, :, 1, :],
                       packed(mask[l][:, :], l)).then_inc(dve_scan, 1)
                if more:
                    taps("w", u + 1, dve_proj, DVE_PROJ)

                def level_scores(l):
                    i = LEVELS[1:].index(l)
                    pe_done(f"s{l}")
                    if i >= 2:
                        dve.wait_ge(pool_scan, after(POOL_SCAN, f"ad{LEVELS[1:][i - 2]}", u))
                    tt(packed(tmp[i % 2][:, 0:T // 2], l), packed(bank[f"s{l}"][:, 0:T // 2], l),
                       halves(F[l][:, :], l)[:, :, 1, :]).then_inc(dve_scan, 1)

                for l in (2, 4, 8):
                    level_scores(l)
                pe_done("U0")
                nc.vector.tensor_copy(state[:, 0, :], bank["U0"][:, 0:2 * P]).then_inc(dve_scan, 1)
                for c in (1, 2):
                    pe_done(f"U{c}")
                    own(f"St{c - 1}")
                    nc.vector.scalar_tensor_tensor(state[:, c, :], state[:, c - 1, :], G[:, (c + 1) * P - 1:(c + 1) * P],
                                                   bank[f"U{c}"][:, 0:2 * P], ALU.mult, ALU.add).then_inc(dve_scan, 1)
                level_scores(16)
                level_scores(32)
                pe_done("sst")
                tt(tmp[2][:, :], bank["sst"][:, 0:T - P], G[:, P:T]).then_inc(dve_scan, 1)
                level_scores(64)
                pe_done("sT")
                nc.vector.tensor_reduce(nmx[:, :], chunks(bank["sT"]), AX.X, ALU.max, negate=True).then_inc(dve_scan, 1)
                own("mx")
                nc.vector.tensor_scalar(nms[:, :], nmx[:, :], SCALE, None, ALU.mult).then_inc(dve_scan, 1)
                if more:
                    taps("k", u + 1, dve_proj, DVE_PROJ)
                dve.wait_ge(act_scan, after(ACT_SCAN, "e3", u))
                nc.vector.reciprocal(rs[:, :], rsum[:, :]).then_inc(dve_scan, 1)
                pe_done("a2d")
                tt(chunks(A2), chunks(bank["a2d"]), eye).then_inc(dve_scan, 1)
                own("a2d")
                for l in LEVELS:
                    pe_done(f"a2_{l}")
                    nc.vector.memset(hold[:, :], 0.0)
                    nc.vector.copy_predicated(halves(A2[:, :], l)[:, :, 1, :], packed(mask[l][:, :], l).bitcast(INT32),
                                              packed(bank[f"a2_{l}"][:, 0:T // 2], l)).then_inc(dve_scan, 1)
                    own(f"a2_{l}")
                if more:
                    taps("v", u + 1, dve_proj, DVE_PROJ)
                dve.wait_ge(act_scan, after(ACT_SCAN, "osq", u))
                nc.vector.tensor_reduce(oss[:, :], sq[:, :, :], AX.X, ALU.add).then_inc(dve_scan, 1)
                if more:
                    for name in F_STEPS[:4]:
                        f_step(u + 1, name)
                dve.wait_ge(pool_scan, after(POOL_SCAN, "r5", u))
                tt(on[:, :, :], chunks(bank["o"]),
                   r5[:, :].rearrange("p (c o) -> p c o", o=1).to_broadcast([P, C, P])).then_inc(dve_scan, 1)
                if more:
                    for name in F_STEPS[4:7]:
                        f_step(u + 1, name)
                pe_done("onT")
                dst = og[:, h, :] if isinstance(h, int) else og[:, bass.ds(h, 1), :].rearrange("p o t -> p (o t)")
                nc.vector.scalar_tensor_tensor(dst, bank["onT"][:, :], norm_w[:, 0:1], sg[:, :],
                                               ALU.mult, ALU.mult).then_inc(dve_scan, 1)
                if more:
                    for name in F_STEPS[7:]:
                        f_step(u + 1, name)

            with dve.Fori(0, NB) as b:
                dve.wait_ge(xn_full, (b + 1) * 16)
                for c in range(C):
                    nc.vector.bn_stats(stats[:, c, :], xn[:, c, :]).then_inc(dve_edge, 1)
                dve.wait_ge(dve_edge, after(DVE_EDGE, "st3", b))
                nc.vector.memset(hold[:, :], 0.0)
                for c in range(C):
                    nc.vector.bn_aggr(mv[:, c, :], stats[:, c, :]).then_inc(dve_edge, 1)
                dve.wait_ge(pool_edge, after(POOL_EDGE, "rstd", b))
                for c in range(C):
                    nc.vector.tensor_scalar(xn[:, c, :], xn[:, c, :], mv[:, c, 0:1], rstd[:, c:c + 1],
                                            ALU.subtract, ALU.mult).then_inc(dve_edge, 1)
                head_taps(b * NH, 0)
                taps("w", b * NH, dve_proj, DVE_PROJ)
                taps("k", b * NH, dve_proj, DVE_PROJ)
                taps("v", b * NH, dve_proj, DVE_PROJ)
                for name in F_STEPS:
                    f_step(b * NH, name)
                with dve.Fori(0, NH - 1) as h:
                    scan(b * NH + h, h, True)
                scan(b * NH + (NH - 1), NH - 1, False)
                dve.wait_ge(pe_edge, after(PE_EDGE, "wo15", b))
                dve.wait_ge(res_full, (b + 1) * 16)
                for c in range(C):
                    nc.vector.tensor_tensor(res[:, c, :], (lv + tb)[c][:, :], res[:, c, :],
                                            ALU.add).then_inc(dve_edge, 1)

        @block.tensor
        def _(pe):
            for steps, done in ((PE_PROJ, pe_proj), (PE_SCAN, pe_scan), (PE_EDGE, pe_edge)):
                pe.sem_inc(done, len(steps))
            pe.wait_ge(pool_consts, 27)
            pe.wait_ge(small_full, 16 * SMALL)

            def arrived(n, unit):
                pe.wait_ge(slot_full[n], (unit + 1) * 16)

            def project(n, kk):
                mm = nc.tensor.matmul(bank[n][:, :], ck_(slot[n], kk), hT[:, kk, :], start=(kk == 0),
                                      stop=(kk == KT - 1))
                if kk == KT - 1:
                    mm.then_inc(pe_proj, 1)

            def project_decay():
                nc.tensor.matmul(bank["g"][:, :], slot["g"][:, :], f1T[:, :], start=True,
                                 stop=True).then_inc(pe_proj, 1)

            def scan(u, more):
                def act_done(name):
                    pe.wait_ge(act_scan, after(ACT_SCAN, name, u))

                def dve_done(name):
                    pe.wait_ge(dve_scan, after(DVE_SCAN, name, u))

                def pool_done(name):
                    pe.wait_ge(pool_scan, after(POOL_SCAN, name, u))

                def transpose(name, src, n=C):
                    for c in range(n):
                        last = nc.tensor.transpose(ck_(bank[name], c), src(c), ident[:, :])
                    last.then_inc(pe_scan, 1)

                def fill(*parts):
                    if more:
                        for n, kk in parts:
                            if kk == 0:
                                arrived(n, u + 1)
                                if n == "w":
                                    act_done("sg")
                                if n == "k":
                                    dve_done("cq3")
                                if n == "v":
                                    pe.wait_ge(dve_proj, after(DVE_PROJ, "cw3", u + 1))
                                if n == "q":
                                    pe.wait_ge(dve_proj, after(DVE_PROJ, "ck3", u + 1))
                            project(n, kk)

                def scores(l):
                    for c in range(C):
                        last = nc.tensor.matmul(ck_(bank[f"s{l}"], c, P // 2), XT[l][:, c, :],
                                                ck_(AM[l], c, P // 2), start=True, stop=True)
                    last.then_inc(pe_scan, 1)

                pe.wait_ge(act_proj, after(ACT_PROJ, "k", u))
                transpose("kT", lambda c: ck_(k, c))
                arrived("gate", u)
                pe.wait_ge(dve_proj, after(DVE_PROJ, "cv3", u))
                nc.tensor.matmul(bank["gate"][:, :], slot["gate"][:, :], g1T[:, :], start=True,
                                 stop=True).then_inc(pe_scan, 1)
                pe.wait_ge(dve_scan, before(DVE_SCAN, u))
                transpose("wT", lambda c: ck_(w, c))
                pool_done("x1")
                transpose("x1T", lambda c: ck_(XS[1], c))
                pool_done("x2")
                act_done("xt0")
                transpose("x2T", lambda c: ck_(XS[2], c))
                fill(("w", 0))
                pool_done("x4")
                act_done("xt1")
                transpose("x4T", lambda c: ck_(XS[4], c))
                fill(("w", 1))
                pool_done("x8")
                act_done("xt2")
                transpose("x8T", lambda c: ck_(XS[8], c))
                fill(("w", 2))
                act_done("v")
                transpose("vT", lambda c: ck_(v, c))
                fill(("w", 3))
                pool_done("x16")
                act_done("xt4")
                dve_done("vr")
                for c in range(C):
                    last = nc.tensor.matmul(ck_(bank["A"], c), ck_(k, c), ck_(q, c), start=True, stop=True)
                last.then_inc(pe_scan, 1)
                transpose("x16T", lambda c: ck_(XS[16], c))
                pool_done("x32")
                act_done("xt8")
                transpose("x32T", lambda c: ck_(XS[32], c))
                pool_done("x64")
                act_done("xt16")
                transpose("x64T", lambda c: ck_(XS[64], c))
                pool_done("b64")
                act_done("xt32")
                transpose("xbT", lambda c: ck_(xb, c), C - 1)
                dve_done("am1")
                for c in range(C):
                    nc.tensor.matmul(ck_(bank["s0"], c), XT[0][:, c, :], ck_(AM[0], c), start=True, stop=False)
                    last = nc.tensor.matmul(halves(ck_(bank["s0"], c), 1)[:, :, 1, 0], XT[1][:, c, :],
                                            ck_(AM[1], c, P // 2), start=False, stop=True)
                last.then_inc(pe_scan, 1)
                dve_done("am2")
                scores(2)
                dve_done("am4")
                act_done("s0")
                scores(4)
                dve_done("m2")
                scores(8)
                act_done("xtb")
                for c in range(C - 1):
                    if c == 2:
                        dve_done("St0")
                    nc.tensor.matmul(bank[f"U{c}"][:, 0:2 * P], XTB[:, c, :], kv[:, c, :], start=True,
                                     stop=True).then_inc(pe_scan, 1)
                dve_done("m4")
                scores(16)
                dve_done("St2")
                act_done("xt64")
                transpose("skT", lambda c: state[:, c, 0:P], C - 1)
                dve_done("m8")
                scores(32)
                act_done("sk")
                dve_done("m16")
                for c in range(C - 1):
                    last = nc.tensor.matmul(ck_(bank["sst"], c), Sk[:, c, :], ck_(q, c + 1), start=True, stop=True)
                last.then_inc(pe_scan, 1)
                dve_done("m32")
                scores(64)
                fill(("k", 0), ("k", 1), ("k", 2), ("k", 3))
                pool_done("ad64")
                transpose("sT", lambda c: ck_(s, c))
                fill(("v", 0), ("v", 1), ("v", 2))
                act_done("e3")
                transpose("aT", lambda c: au[:, c, :])
                fill(("v", 3))
                act_done("aT")
                for c in range(C):
                    last = nc.tensor.matmul(ck_(bank["a2d"], c), ck_(w, c), ck_(aT, c), start=True, stop=True)
                last.then_inc(pe_scan, 1)
                for c in range(C):
                    last = nc.tensor.matmul(ck_(bank["a2_1"], c, P // 2), ck_(XS[1], c),
                                            halves(ck_(aT, c), 1)[:, :, 1, 0], start=True, stop=True)
                last.then_inc(pe_scan, 1)
                for l in LEVELS[1:]:
                    pool_done(f"y{l}")
                    dve_done("a2d" if l == 2 else f"a2_{l // 4}")
                    for c in range(C):
                        last = nc.tensor.matmul(ck_(bank[f"a2_{l}"], c, P // 2), ck_(XS[l], c),
                                                ck_(Y[l], c, P // 2), start=True, stop=True)
                    last.then_inc(pe_scan, 1)
                if more:
                    arrived("g", u + 1)
                    project_decay()
                dve_done("a2_64")
                pool_done("yst")
                for c in range(C):
                    last = nc.tensor.matmul(ck_(bank["o"], c), ck_(A2, c), kv[:, c, P:2 * P], start=True, stop=(c == 0))
                    if c:
                        last = nc.tensor.matmul(ck_(bank["o"], c), ck_(Yst, c - 1), state[:, c - 1, P:2 * P],
                                                start=False, stop=True)
                last.then_inc(pe_scan, 1)
                fill(("q", 0), ("q", 1), ("q", 2), ("q", 3))
                dve_done("on")
                transpose("onT", lambda c: on[:, c, :])

            with pe.Fori(0, NB) as b:
                pe.wait_ge(dve_edge, after(DVE_EDGE, "xn3", b))
                for kk in range(KT):
                    for c in range(C):
                        last = nc.tensor.transpose(ck_((lv + tb)[kk], c), xn[:, c, kk * P:(kk + 1) * P], ident[:, :])
                    last.then_inc(pe_edge, 1)
                pe.wait_ge(act_edge, after(ACT_EDGE, "hT3", b))
                for dst, wt in ((mi[0], wf1), (mi[1], wg1)):
                    for kk in range(KT):
                        last = nc.tensor.matmul(dst[:, :], wt[:, kk, :], hT[:, kk, :], start=(kk == 0),
                                                stop=(kk == KT - 1))
                    last.then_inc(pe_edge, 1)
                for c in range(C):
                    for kk in range(KT):
                        last = nc.tensor.matmul(pr[0][:, c * NH:(c + 1) * NH], ck_(hT[:, kk, :], c), wb[:, kk, :],
                                                start=(kk == 0), stop=(kk == KT - 1))
                last.then_inc(pe_edge, 1)
                pe.wait_ge(act_edge, after(ACT_EDGE, "beta", b))
                n = b * NH
                arrived("w", n)
                for kk in range(KT):
                    project("w", kk)
                arrived("k", n)
                for kk in range(KT):
                    project("k", kk)
                arrived("v", n)
                pe.wait_ge(dve_proj, after(DVE_PROJ, "cw3", n))
                for kk in range(KT):
                    project("v", kk)
                arrived("g", n)
                project_decay()
                arrived("q", n)
                pe.wait_ge(dve_proj, after(DVE_PROJ, "ck3", n))
                for kk in range(KT):
                    project("q", kk)
                with pe.Fori(0, NH - 1) as h:
                    scan(b * NH + h, True)
                scan(b * NH + (NH - 1), False)
                pe.wait_ge(dve_scan, before(DVE_SCAN, (b + 1) * NH))
                for h in range(NH):
                    pe.wait_ge(wo_full[h % 4], b * (16 * NH // 4) + 16 * (h // 4 + 1))
                    for c in range(C):
                        last = nc.tensor.matmul((lv + tb)[c][:, :], ck_(og[:, h, :], c), wo[h % 4][:, :],
                                                start=(h == 0), stop=(h == NH - 1))
                    last.then_inc(pe_edge, 1)


def build(nc, a, out):
    x1 = nc.dram_tensor("x1", (NB * T, HID), FP32, kind="Internal").ap()
    x2 = nc.dram_tensor("x2", (NB * T, HID), FP32, kind="Internal").ap()
    wq_dram = nc.dram_tensor("wq_dram", (3, P, KT * FF), FP32, kind="Internal").ap()
    ffn_w = (a["w1"], a["w2"], a["w3"])
    ffn_phase(nc, True, a["x"], x1, ffn_w, wq_dram)
    attention_phase(nc, x1, x2, a)
    ffn_phase(nc, False, x2, out, ffn_w, wq_dram)


def kernel(**inputs):
    import numpy as _np
    import concourse.bacc as _bacc
    from concourse import mybir as _mybir
    from concourse.bass_utils import run_bass_kernel_spmd as _run

    a = {k[3:]: _np.asarray(v) for k, v in inputs.items()}

    def heads_first(w):
        k = w.shape[0] // 128
        return w.reshape(k, 128, 16, 128).transpose(2, 1, 0, 3).reshape(16, 128, k * 128)

    def channels(w):
        return w.reshape(16, 128, -1).transpose(1, 0, 2)

    laid = {
        "x": a["attn_hidden_states"].reshape(2048, 512),
        "wq": heads_first(a["attn_Wq"]), "wk": heads_first(a["attn_Wk"]),
        "wv": heads_first(a["attn_Wv"]), "ww": heads_first(a["attn_Ww"]),
        "wf2": heads_first(a["attn_Wf2"]), "wg2": heads_first(a["attn_Wg2"]),
        "per_head": _np.concatenate([channels(a[f"attn_{n}"]) for n in ("cq", "ck", "cv", "bg2")], axis=2),
        "norm_w": a["attn_norm_w"].reshape(128, 1),
        "wf1": a["attn_Wf1"], "wg1": a["attn_Wg1"], "wb": a["attn_Wb"],
        "wo": a["attn_Wo"].reshape(16, 128, 512),
        "w1": a["ffn_w1"].T, "w2": a["ffn_w2"].T, "w3": a["ffn_w3"].T,
    }
    nc = _bacc.Bacc("TRN2", target_bir_lowering=False, num_devices=1)
    arrays, args = {}, {}
    for name, v in laid.items():
        v = _np.ascontiguousarray(v)
        arrays[f"in_{name}_dram"] = v
        args[name] = nc.dram_tensor(f"in_{name}_dram", v.shape, _mybir.dt.from_np(v.dtype), kind="ExternalInput").ap()
    out = nc.dram_tensor("out_dram", (2048, 512), _mybir.dt.float32, kind="ExternalOutput").ap()
    build(nc, args, out)
    r = _run(nc, [arrays], core_ids=[0])
    return r.results[0]["out_dram"].reshape(4, 512, 512)
```

```python
from contextlib import ExitStack

import concourse.bass as bass
from concourse import mybir
from concourse.alu_op_type import AluOpType as ALU

FP32 = mybir.dt.float32
F32R = mybir.dt.float32r
INT32 = mybir.dt.int32
ACT = mybir.ActivationFunctionType
AX = mybir.AxisListType

P = 128
NB, T, HID = 4, 512, 512
NH = 16
FF = 1408
C = T // P
KT = HID // P
MT = FF // P
KW = 4
LEVELS = [1, 2, 4, 8, 16, 32, 64]
SCALE = P ** -0.5
LN_EPS = 1e-5
L2_EPS = 1e-6
RMS_EPS = 1e-5
Q_EPS = 1e-8


def halves(ap, level):
    return ap.rearrange("p (n two l) -> p n two l", two=2, l=level)


def packed(ap, level):
    return ap.rearrange("p (n l) -> p n l", l=level)


def ffn_phase(nc, first, x_in, x_out, w_t, wq_dram):
    with ExitStack() as ctx:
        def sb(name, shape, dt=FP32):
            return ctx.enter_context(nc.sbuf_tensor(f"{name}_{int(first)}", shape, dt))

        def sem(name):
            return ctx.enter_context(nc.semaphore(f"{name}_{int(first)}"))

        wq = [sb(f"wq{i}", [P, KT * FF], F32R) for i in range(3)]
        up = [wq[i][:, :].rearrange("p (k n) -> p k n", k=KT) for i in range(2)]
        down = wq[2][:, :].rearrange("p (m n) -> p m n", m=MT)
        x_sb = sb("x_sb", [P, NB * C, HID])
        x_new = sb("x_new", [P, C, HID])
        xn = sb("xn", [P, C, HID])
        stats = sb("stats", [P, C, 6])
        mv = sb("mv", [P, C, 2])
        gate = sb("gate", [P, 1])
        rstd = sb("rstd", [P, C])
        ve = sb("ve", [P, C])
        eps_t = sb("eps_t", [P, C])
        mhalf = sb("mhalf", [P, C])
        ident = sb("ident", [P, P])
        ones = sb("ones", [P, P])
        h_hi = sb("h_hi", [P, KT, T], F32R)
        h_lo = sb("h_lo", [P, KT, T], F32R)
        sig = sb("sig", [P, 2, T])
        hid = sb("hid", [P, 2, T])
        g_hi = [sb(f"g_hi{i}", [P, T], F32R) for i in range(2)]
        g_lo = [sb(f"g_lo{i}", [P, T], F32R) for i in range(2)]
        if first:
            raw = [sb(f"raw{i}", [P, KT * FF]) for i in range(2)]
            below = sb("below", [P, FF])
            junk = sb("junk", [P, FF])
            asum = sb("asum", [P, 3, KT])
            tot = sb("tot", [P, 3])
            gamma = sb("gamma", [P, 3])
            thr = sb("thr", [P, 3])
            nthr = sb("nthr", [P, 3])
        up_ps = [[ctx.enter_context(nc.psum_tensor(f"up_ps{i}{j}_{int(first)}", [P, T], FP32)) for j in range(2)]
                 for i in range(2)]
        out_ps = [ctx.enter_context(nc.psum_tensor(f"out_ps{c}_{int(first)}", [P, HID], FP32)) for c in range(C)]

        consts_ready = sem("consts_ready")
        raw_full = [sem(f"raw_full{i}") for i in range(3)]
        abs_summed = sem("abs_summed")
        total_ready = sem("total_ready")
        thr_step = sem("thr_step")
        below_ready = sem("below_ready")
        quantised = sem("quantised")
        wq_saved = sem("wq_saved")
        groups = [(m, min(m + 3, MT)) for m in range(0, MT, 3)]
        wq_full = [[sem(f"wq_full{i}{j}") for j in range(len(groups))] for i in range(3)]
        x_full = sem("x_full")
        stats_step = sem("stats_step")
        rstd_step = sem("rstd_step")
        xn_ready = sem("xn_ready")
        ln_transposed = sem("ln_transposed")
        h_split = sem("h_split")
        gate_in = sem("gate_in")
        value_in = sem("value_in")
        sig_ready = sem("sig_ready")
        hid_step = sem("hid_step")
        down_done = sem("down_done")
        out_added = sem("out_added")
        out_stored = sem("out_stored")
        block = ctx.enter_context(nc.Block())

        @block.sync
        def _(sp):
            def rows(dram, b):
                return dram[b * T:(b + 1) * T, :].rearrange("(c p) d -> p c d", p=P)

            sp.sem_inc(out_stored, 16)
            sp.dma_start(x_sb[:, 0:C, :], rows(x_in, 0)).then_inc(x_full, 16)

            def load_quantised(i, j):
                m0, m1 = groups[j]
                if i < 2:
                    part = [t.rearrange("p (k n) -> p k n", k=KT)[:, :, m0 * P:m1 * P]
                            for t in (wq[i][:, :].bitcast(FP32), wq_dram[i, :, :])]
                else:
                    part = [wq[i][:, m0 * HID:m1 * HID].bitcast(FP32), wq_dram[i, :, m0 * HID:m1 * HID]]
                sp.dma_start(*part).then_inc(wq_full[i][j], 16)

            for i in range(2):
                if first:
                    sp.dma_start(raw[i][:, :].rearrange("p (k n) -> p k n", k=KT),
                                 w_t[i].rearrange("(k p) n -> p k n", p=P)).then_inc(raw_full[i], 16)

            def load_rows(b):
                sp.wait_ge(x_full, 16 * b)
                sp.dma_start(x_sb[:, b * C:(b + 1) * C, :], rows(x_in, b)).then_inc(x_full, 16)

            if not first:
                for j in range(len(groups)):
                    for i in range(3):
                        load_quantised(i, j)
                    if j == 1:
                        load_rows(1)
            if first:
                sp.wait_ge(quantised, KT)
                sp.dma_start(raw[0][:, :].rearrange("p (m n) -> p m n", m=MT),
                             w_t[2].rearrange("(m p) n -> p m n", p=P)).then_inc(raw_full[2], 16)
                load_rows(1)
                for i in range(3):
                    sp.wait_ge(quantised, KT * (i + 1))
                    sp.dma_start(wq_dram[i, :, :], wq[i][:, :].bitcast(FP32)).then_inc(wq_saved, 16)
            for b in range(2, NB):
                load_rows(b)
            with sp.Fori(0, NB) as b:
                sp.wait_ge(out_added, C * b + 2 * C)
                sp.dma_start(x_out[bass.ds(b * T, T), :].rearrange("(c p) d -> p c d", p=P),
                             x_new[:, :, :]).then_inc(out_stored, 16)
            sp.wait_ge(out_stored, 16 * NB + 16)
            if first:
                sp.wait_ge(wq_saved, 48)

        @block.gpsimd
        def _(pool):
            nc.gpsimd.memset(ident[:, :], 0.0).then_inc(consts_ready, 1)
            nc.gpsimd.memset(ones[:, :], 1.0).then_inc(consts_ready, 1)
            nc.gpsimd.memset(eps_t[:, :], LN_EPS).then_inc(consts_ready, 1)
            nc.gpsimd.memset(mhalf[:, :], -0.5).then_inc(consts_ready, 1)
            pool.wait_ge(consts_ready, 4)
            nc.gpsimd.affine_select(out=ident[:, :], in_=ident[:, :], compare_op=ALU.not_equal, fill=1.0, base=0,
                                    pattern=[[-1, P]], channel_multiplier=1).then_inc(consts_ready, 1)

            def deviation(i):
                pool.wait_ge(stats_step, 8 * i + 8)
                nc.gpsimd.tensor_tensor(ve[:, :], mv[:, :, 1], eps_t[:, :], ALU.add).then_inc(rstd_step, 1)
                pool.wait_ge(rstd_step, 2 * i + 1)
                nc.gpsimd.tensor_tensor(rstd[:, :], ve[:, :], mhalf[:, :], ALU.pow).then_inc(rstd_step, 1)

            deviation(0)
            with pool.Fori(1, NB) as i:
                deviation(i)

        @block.scalar
        def _(act):
            if first:
                for i in range(3):
                    act.wait_ge(raw_full[i], 16)
                    for k in range(KT):
                        nc.scalar.activation(junk[:, :], raw[i % 2][:, k * FF:(k + 1) * FF], ACT.Abs,
                                             accum_out=asum[:, i, k:k + 1]).then_inc(abs_summed, 1)
                        act.wait_ge(abs_summed, KT * i + k + 1)
            with act.Fori(0, NB) as b:
                for m in range(MT):
                    act.wait_ge(gate_in, MT * b + m + 1)
                    if m >= 2:
                        act.wait_ge(hid_step, 3 * (MT * b + m - 2 + MT) + 1)
                    nc.scalar.activation(sig[:, m % 2, :], up_ps[0][m % 2][:, :],
                                         ACT.Sigmoid).then_inc(sig_ready, 1)

        @block.vector
        def _(dve):
            def norm_stats(i):
                dve.wait_ge(x_full, 16 * i + 16)
                nc.vector.memset(gate[:, :], 0.0)
                for c in range(C):
                    nc.vector.bn_stats(stats[:, c, :], x_rows(i, c)).then_inc(stats_step, 1)
                dve.wait_ge(stats_step, 8 * i + C)
                nc.vector.memset(gate[:, :], 0.0)
                for c in range(C):
                    nc.vector.bn_aggr(mv[:, c, :], stats[:, c, :]).then_inc(stats_step, 1)

            def x_rows(i, c):
                if isinstance(i, int):
                    return x_sb[:, i * C + c, :]
                return x_sb[:, bass.ds(i * C + c, 1), :].rearrange("p o d -> p (o d)")

            def norm_apply(i):
                dve.wait_ge(rstd_step, 2 * i + 2)
                if not isinstance(i, int):
                    dve.wait_ge(ln_transposed, KT * i)
                for c in range(C):
                    nc.vector.tensor_scalar(xn[:, c, :], x_rows(i, c), mv[:, c, 0:1], rstd[:, c:c + 1],
                                            ALU.subtract, ALU.mult).then_inc(xn_ready, 1)

            dve.sem_inc(hid_step, 3 * MT)
            dve.sem_inc(out_added, C)
            norm_stats(0)
            norm_apply(0)
            if first:
                for i in range(3):
                    s = 4 * i
                    dve.wait_ge(total_ready, i + 1)
                    nc.vector.tensor_reduce(tot[:, i:i + 1], out_ps[i][:, 0:KT], AX.X, ALU.add).then_inc(thr_step, 1)
                    dve.wait_ge(thr_step, s + 1)
                    nc.vector.tensor_scalar(gamma[:, i:i + 1], tot[:, i:i + 1], 1.0 / (FF * HID), Q_EPS,
                                            ALU.mult, ALU.add).then_inc(thr_step, 1)
                    dve.wait_ge(thr_step, s + 2)
                    nc.vector.tensor_scalar(nthr[:, i:i + 1], gamma[:, i:i + 1], -0.5, None,
                                            ALU.mult).then_inc(thr_step, 1)
                    nc.vector.tensor_scalar(thr[:, i:i + 1], gamma[:, i:i + 1], 0.5, None,
                                            ALU.mult).then_inc(thr_step, 1)
                    dve.wait_ge(thr_step, s + 4)
                    for k in range(KT):
                        piece = slice(k * FF, (k + 1) * FF)
                        dve.wait_ge(quantised, KT * i + k)
                        nc.vector.tensor_scalar(below[:, :], raw[i % 2][:, piece], nthr[:, i:i + 1], None,
                                                ALU.is_lt).then_inc(below_ready, 1)
                        dve.wait_ge(below_ready, KT * i + k + 1)
                        nc.vector.scalar_tensor_tensor(wq[i][:, piece], raw[i % 2][:, piece], thr[:, i:i + 1],
                                                       below[:, :], ALU.is_gt, ALU.subtract).then_inc(quantised, 1)

            def split_norm(b):
                for k in range(KT):
                    bank = up_ps[k // 2][k % 2]
                    dve.wait_ge(ln_transposed, KT * b + k + 1)
                    nc.vector.tensor_copy(h_hi[:, k, :], bank[:, :]).then_inc(h_split, 1)
                    dve.wait_ge(h_split, 2 * (KT * b + k) + 1)
                    nc.vector.tensor_tensor(h_lo[:, k, :], bank[:, :], h_hi[:, k, :].bitcast(FP32),
                                            ALU.subtract).then_inc(h_split, 1)

            def batch(b, last):
                split_norm(b)
                for m in range(MT):
                    n = MT * b + m
                    dve.wait_ge(sig_ready, n + 1)
                    dve.wait_ge(value_in, n + 1)
                    nc.vector.tensor_tensor(hid[:, m % 2, :], up_ps[1][m % 2][:, :], sig[:, m % 2, :],
                                            ALU.mult).then_inc(hid_step, 1)
                    dve.wait_ge(hid_step, 3 * (n + MT) + 1)
                    if m >= 2:
                        dve.wait_ge(down_done, n - 1)
                    nc.vector.tensor_copy(g_hi[m % 2][:, :], hid[:, m % 2, :]).then_inc(hid_step, 1)
                    dve.wait_ge(hid_step, 3 * (n + MT) + 2)
                    nc.vector.tensor_tensor(g_lo[m % 2][:, :], hid[:, m % 2, :], g_hi[m % 2][:, :].bitcast(FP32),
                                            ALU.subtract).then_inc(hid_step, 1)
                    if m == 3 and not last:
                        norm_stats(b + 1)
                    if m == 5 and not last:
                        norm_apply(b + 1)
                dve.wait_ge(down_done, MT * b + MT)
                dve.wait_ge(out_stored, 16 * b + 16)
                for c in range(C):
                    nc.vector.scalar_tensor_tensor(x_new[:, c, :], out_ps[c][:, :], 0.5, x_rows(b, c),
                                                   ALU.mult, ALU.add).then_inc(out_added, 1)

            with dve.Fori(0, NB - 1) as b:
                batch(b, False)
            batch(NB - 1, True)

        @block.tensor
        def _(pe):
            pe.wait_ge(consts_ready, 5)
            if first:
                for i in range(3):
                    pe.wait_ge(abs_summed, KT * (i + 1))
                    nc.tensor.matmul(out_ps[i][:, 0:KT], ones[:, :], asum[:, i, :], start=True,
                                     stop=True).then_inc(total_ready, 1)
                pe.wait_ge(quantised, 3 * KT)

            def down_tile(b, m):
                pe.wait_ge(hid_step, 3 * (MT * b + m + MT) + 3)
                if m == 0:
                    pe.wait_ge(out_added, C * b + C)
                for c in range(C):
                    for part in (g_hi, g_lo):
                        last = nc.tensor.matmul(out_ps[c][:, :], part[m % 2][:, c * P:(c + 1) * P], down[:, m, :],
                                                start=(m == 0 and part is g_hi),
                                                stop=(m == MT - 1 and part is g_lo))
                last.then_inc(down_done, 1)

            with pe.Fori(0, NB) as b:
                pe.wait_ge(xn_ready, C * b + C)
                pe.wait_ge(hid_step, 3 * MT * b + 3 * MT)
                for k in range(KT):
                    for c in range(C):
                        last = nc.tensor.transpose(up_ps[k // 2][k % 2][:, c * P:(c + 1) * P],
                                                   xn[:, c, k * P:(k + 1) * P], ident[:, :])
                    last.then_inc(ln_transposed, 1)
                pe.wait_ge(h_split, 2 * KT * (b + 1))
                for m in range(MT):
                    if not first and m % 3 == 0:
                        for i in range(3):
                            pe.wait_ge(wq_full[i][m // 3], 16)
                    if m >= 2:
                        pe.wait_ge(hid_step, 3 * (MT * b + m - 2 + MT) + 1)
                    for which, ready in ((0, gate_in), (1, value_in)):
                        for k in range(KT):
                            for part in (h_hi, h_lo):
                                last = nc.tensor.matmul(up_ps[which][m % 2][:, :],
                                                        up[which][:, k, m * P:(m + 1) * P], part[:, k, :],
                                                        start=(k == 0 and part is h_hi),
                                                        stop=(k == KT - 1 and part is h_lo))
                        last.then_inc(ready, 1)
                    if m >= 1:
                        down_tile(b, m - 1)
                down_tile(b, MT - 1)


PE_PROJ = "w k v g q gate wT".split()
PE_SCAN = ("kT x1T x2T x4T A x8T x16T x32T vT x64T xbT s0 s2 U0 U1 s4 s8 U2 s16 skT s32 sst s64 sT aT "
           "a2d a2_1 a2_2 a2_4 a2_8 a2_16 a2_32 a2_64 o onT").split()
ACT_PROJ = "acc_w acc_k acc_v w xb k v g acc_q sq xt0".split()
ACT_SCAN = "sg xt1 q xt2 xt4 xt8 xt16 xt32 xt64 xtb s0 sk e0 e1 e2 e3 aT osq".split()
DVE_PROJ = ("tap cw1 cw2 cw3 ck1 ck2 ck3 cv1 cv2 cv3 f2 c2 f4 c4 f8 ss cq1 c8 cq2 cq3 f16 c16 f32 c32 f64").split()
DVE_SCAN = ("kr As am0 am1 am2 vr am4 am8 am16 am32 am64 c64 f128 G m2 St0 St1 m4 St2 m8 m16 m32 mst m64 mx nms "
            "rs a2d a2_1 a2_2 a2_4 a2_8 a2_16 a2_32 a2_64 oss on og").split()
POOL_SCAN = ("x1 b1 x2 b2 x4 b4 x8 bne bnp bn b8 x16 b16 x32 b32 x64 b64 ad2 ad4 ad8 ad16 ad32 adst ad64 "
             "y2 y4 y8 y16 y32 y64 yst r1 r2 r3 r4 r5").split()
PE_EDGE = "lnT0 lnT1 lnT2 lnT3 f1 g1 beta".split()
PE_OUT = [f"wo{h}" for h in range(NH - 1)] + "o0 o1 o2 o3".split()
ACT_EDGE = "hT0 hT1 hT2 hT3 f1 g1 beta".split()
DVE_EDGE = "st0 st1 st2 st3 ag0 ag1 ag2 ag3 xn0 xn1 xn2 xn3".split()
DVE_OUT = "add0 add1 add2 add3".split()
POOL_EDGE = "ve rstd".split()


def after(steps, name, u):
    return u * len(steps) + (len(steps) + steps.index(name) + 1)


def before(steps, u):
    return u * len(steps) + len(steps)


def attention_phase(nc, x_in, x_out, a):
    with ExitStack() as ctx:
        def sb(name, shape, dt=FP32):
            return ctx.enter_context(nc.sbuf_tensor(name, shape, dt))

        def ps(name, width=T):
            return ctx.enter_context(nc.psum_tensor(name, [P, width], FP32))

        def sem(name):
            return ctx.enter_context(nc.semaphore(name))

        ident = sb("ident", [P, P])
        mask = {l: sb(f"mask{l}", [P, T // 2]) for l in LEVELS}
        l2_eps = sb("l2_eps", [P, C])
        rms_eps = sb("rms_eps", [P, C])
        ln_eps = sb("ln_eps", [P, C])
        mhalf = sb("mhalf_a", [P, C])
        hold = sb("hold", [P, 1])
        wf1 = sb("wf1", [P, KT, P])
        wg1 = sb("wg1", [P, KT, P])
        wb = sb("wb", [P, KT, NH])
        per_head = sb("per_head", [P, NH, 3 * KW + 1])
        norm_w = sb("norm_w", [P, 1])
        slot = {n: sb(f"slot_{n}", [P, HID]) for n in "wkvq"}
        slot["g"] = sb("slot_g", [P, P])
        slot["gate"] = sb("slot_gate", [P, P])
        wo = [sb(f"wo{i}", [P, HID]) for i in range(4)]
        xn = sb("xn_a", [P, C, HID])
        res = sb("res", [P, C, HID])
        stats = sb("stats_a", [P, C, 6])
        mv = sb("mv_a", [P, C, 2])
        ve = sb("ve_a", [P, C])
        rstd = sb("rstd_a", [P, C])
        hT = sb("hT", [P, KT, T])
        f1T = sb("f1T", [P, T])
        g1T = sb("g1T", [P, T])
        beta = sb("beta", [P, C, NH])
        og = sb("og", [P, NH, T])
        tap = sb("tap", [P, 3 * KW + 1])
        TAP = {"q": 0, "k": KW, "v": 2 * KW, "w": 2 * KW}
        BIAS = 3 * KW
        acc = {n: sb(f"acc_{n}", [P, T]) for n in "wkvq"}
        w, k, v, q, g, sg, xb = (sb(f"u_{n}", [P, T]) for n in "w k v q g sg xb".split())
        F = {l: sb(f"F{l}", [P, T]) for l in LEVELS[1:] + [P]}
        cc = {l: sb(f"cc{l}", [P, T // (2 * l), 2]) for l in LEVELS[1:]}
        G = sb("G", [P, T])
        XS = {l: sb(f"XS{l}", [P, T]) for l in LEVELS}
        XT = {l: sb(f"XT{l}", [P, C, P]) for l in [0] + LEVELS}
        XTB = sb("XTB", [P, C - 1, P])
        sq = sb("sq", [P, C, P])
        ss = sb("ss", [P, C])
        bn1, bn2, bn = (sb(n, [P, C]) for n in ("bn1", "bn2", "bn"))
        kv = sb("kv", [P, C, 2 * P])
        As = sb("As", [P, T])
        AM = {l: sb(f"AM{l}", [P, T // 2]) for l in LEVELS}
        AM[0] = sb("AM0", [P, T])
        tmp = [sb(f"tmp{i}", [P, T // 2]) for i in range(2)] + [sb("tmp2", [P, T - P])]
        state = sb("state", [P, C - 1, 2 * P])
        Sk = sb("Sk", [P, C - 1, P])
        s = sb("s", [P, T])
        nmx, nms, rsum, rs, oss = (sb(n, [P, C]) for n in "nmx nms rsum rs oss".split())
        r1, r2, r3, r4, r5 = (sb(n, [P, C]) for n in "r1 r2 r3 r4 r5".split())
        au = sb("au", [P, C, P])
        aT = sb("aT", [P, T])
        Y = {l: sb(f"Y{l}", [P, T // 2]) for l in LEVELS[1:]}
        Yst = sb("Yst", [P, T - P])
        A2 = sb("A2", [P, T])
        on = sb("on", [P, C, P])

        pr = [ps(f"pr{i}") for i in range(2)]
        tb = [ps(f"tb{i}") for i in range(2)]
        lv = [ps(f"lv{i}") for i in range(2)]
        mi = [ps(f"mi{i}") for i in range(2)]

        pe_proj, pe_scan, pe_edge = sem("pe_proj"), sem("pe_scan"), sem("pe_edge")
        act_proj, act_scan, act_edge = sem("act_proj"), sem("act_scan"), sem("act_edge")
        dve_proj, dve_scan, dve_edge = sem("dve_proj"), sem("dve_scan"), sem("dve_edge")
        pool_scan, pool_edge, pool_consts = sem("pool_scan"), sem("pool_edge"), sem("pool_consts")
        dve_consts = sem("dve_consts")
        pe_out, dve_out = sem("pe_out"), sem("dve_out")
        small_full = sem("small_full")
        slot_full = {n: sem(f"slot_full_{n}") for n in slot}
        wo_full = [sem(f"wo_full{i}") for i in range(4)]
        xn_full, res_full, res_stored = sem("xn_full"), sem("res_full"), sem("res_stored")
        block = ctx.enter_context(nc.Block())
        SMALL = 5
        bank = {"wT": tb[0], "x1T": tb[1], "x2T": tb[0], "x4T": tb[1], "x8T": tb[0], "x16T": tb[1], "x32T": tb[0],
                "vT": tb[1], "x64T": tb[0], "xbT": tb[1], "skT": tb[0], "sT": tb[1], "aT": tb[0], "onT": tb[1],
                "s0": lv[0], "s2": lv[1], "s4": lv[0], "s8": lv[1], "s16": lv[0], "s32": lv[1], "sst": lv[0],
                "s64": lv[1], "a2d": lv[0], "a2_1": lv[1], "a2_2": lv[0], "a2_4": lv[1], "a2_8": lv[0],
                "a2_16": lv[1], "a2_32": lv[0], "a2_64": lv[1],
                "kT": mi[0], "U0": mi[0], "U2": mi[0], "o": mi[0], "A": mi[1], "U1": mi[1],
                "g": mi[1], "w": pr[0], "v": pr[0], "gate": pr[0], "k": pr[1], "q": pr[1]}

        edge_bank = {"lnT0": pr[0], "lnT1": pr[1], "lnT2": pr[0], "lnT3": pr[1], "f1": pr[0], "g1": pr[1],
                     "beta": mi[1]}
        out_bank = [tb[1], mi[0], lv[0], lv[1]]

        def ck_(t, c, width=P):
            return t[:, c * width:(c + 1) * width]

        def chunks(t):
            return t[:, :].rearrange("p (c n) -> p c n", c=C)

        def rows(dram, b):
            r = dram[b * T:(b + 1) * T, :] if isinstance(b, int) else dram[bass.ds(b * T, T), :]
            return r.rearrange("(c p) d -> p c d", p=P)

        @block.sync
        def _(sp):
            def load_slots(n, u, h):
                src = {"w": a["ww"], "k": a["wk"], "g": a["wf2"], "v": a["wv"], "q": a["wq"], "gate": a["wg2"]}[n]
                src = src[h, :, :] if isinstance(h, int) else src[bass.ds(h, 1), :, :].rearrange("o p n -> (o p) n")
                if u is not None:
                    sp.wait_ge(pe_proj, after(PE_PROJ, n, u))
                sp.dma_start(slot[n][:, :], src).then_inc(slot_full[n], 16)

            sp.sem_inc(res_stored, 16)
            sp.dma_start(xn[:, :, :], rows(x_in, 0)).then_inc(xn_full, 16)
            for dst, src in ((wf1, a["wf1"]), (wg1, a["wg1"]), (wb, a["wb"])):
                sp.dma_start(dst[:, :, :], src.rearrange("(k p) n -> p k n", p=P)).then_inc(small_full, 16)
            sp.dma_start(per_head[:, :, :], a["per_head"]).then_inc(small_full, 16)
            sp.dma_start(norm_w[:, :], a["norm_w"]).then_inc(small_full, 16)
            for n in ("w", "k", "v", "g", "q", "gate"):
                load_slots(n, None, 0)

            def batch(b, final):
                if not final:
                    sp.wait_ge(pe_edge, after(PE_EDGE, "lnT3", b))
                    sp.dma_start(xn[:, :, :], rows(x_in, b + 1)).then_inc(xn_full, 16)
                with sp.Fori(0, NH - 1) as h:
                    for n in ("w", "k", "v", "g", "q", "gate"):
                        load_slots(n, b * NH + h, h + 1)
                if not final:
                    for n in ("w", "k", "v", "g", "q", "gate"):
                        load_slots(n, b * NH + (NH - 1), 0)
                sp.wait_ge(res_stored, b * 16 + 16)
                sp.dma_start(res[:, :, :], rows(x_in, b)).then_inc(res_full, 16)
                for h in range(NH):
                    if h >= 4:
                        sp.wait_ge(pe_out, after(PE_OUT, f"wo{h - 4}", b))
                    else:
                        sp.wait_ge(pe_out, before(PE_OUT, b))
                    sp.dma_start(wo[h % 4][:, :], a["wo"][h, :, :]).then_inc(wo_full[h % 4], 16)
                sp.wait_ge(dve_out, after(DVE_OUT, "add3", b))
                sp.dma_start(rows(x_out, b), res[:, :, :]).then_inc(res_stored, 16)

            with sp.Fori(0, NB - 1) as b:
                batch(b, False)
            batch(NB - 1, True)
            sp.wait_ge(res_stored, 16 * NB + 16)

        @block.gpsimd
        def _(pool):
            for steps, done in ((POOL_SCAN, pool_scan), (POOL_EDGE, pool_edge)):
                pool.sem_inc(done, len(steps))
            nc.gpsimd.memset(ident[:, :], 0.0).then_inc(pool_consts, 1)
            nc.gpsimd.memset(l2_eps[:, :], L2_EPS).then_inc(pool_consts, 1)
            nc.gpsimd.memset(rms_eps[:, :], RMS_EPS).then_inc(pool_consts, 1)
            nc.gpsimd.memset(ln_eps[:, :], LN_EPS).then_inc(pool_consts, 1)
            nc.gpsimd.memset(mhalf[:, :], -0.5).then_inc(pool_consts, 1)
            for l in LEVELS:
                nc.gpsimd.memset(mask[l][:, :], 1.0).then_inc(pool_consts, 1)
            pool.wait_ge(pool_consts, 12)
            nc.gpsimd.affine_select(out=ident[:, :], in_=ident[:, :], compare_op=ALU.not_equal, fill=1.0, base=0,
                                    pattern=[[-1, P]], channel_multiplier=1).then_inc(pool_consts, 1)
            for i, l in enumerate(LEVELS):
                m4 = mask[l][:, :].rearrange("p (c n l) -> p c n l", c=C, l=l)
                blocks = P // (2 * l)
                nc.gpsimd.affine_select(out=m4, in_=m4, compare_op=ALU.is_ge, fill=0.0, base=0,
                                        pattern=[[0, C], [-2 * l, blocks], [0, l]],
                                        channel_multiplier=1).then_inc(pool_consts, 1)
                pool.wait_ge(pool_consts, 14 + 2 * i)
                nc.gpsimd.affine_select(out=m4, in_=m4, compare_op=ALU.is_ge, fill=0.0, base=l - 1,
                                        pattern=[[0, C], [2 * l, blocks], [0, l]],
                                        channel_multiplier=-1).then_inc(pool_consts, 1)
            pool.wait_ge(pool_consts, 27)
            pool.wait_ge(small_full, 16 * SMALL)
            pool.wait_ge(dve_consts, 14)

            def tt(out, in0, in1, op=ALU.mult, done=pool_scan):
                return nc.gpsimd.tensor_tensor(out, in0, in1, op)

            def deviation(b):
                pool.wait_ge(dve_edge, after(DVE_EDGE, "ag3", b))
                tt(ve[:, :], mv[:, :, 1], ln_eps[:, :], ALU.add).then_inc(pool_edge, 1)
                pool.wait_ge(pool_edge, after(POOL_EDGE, "ve", b))
                tt(rstd[:, :], ve[:, :], mhalf[:, :], ALU.pow).then_inc(pool_edge, 1)

            def scan(u, h, batch_next=None):
                def own(name):
                    pool.wait_ge(pool_scan, after(POOL_SCAN, name, u))

                gh = {l: halves(g[:, :], l) for l in LEVELS}

                def decay_to_target(l):
                    return gh[l][:, :, 1, 0:1].to_broadcast([P, T // (2 * l), l])

                pool.wait_ge(act_proj, after(ACT_PROJ, "g", u))
                pool.wait_ge(pe_scan, u * len(PE_SCAN) + PE_SCAN.index("a2_64") + 1)
                prev = None
                for l in LEVELS:
                    if l == 1:
                        src = halves(w[:, :], 1)[:, :, 0, :]
                    else:
                        src = halves(xb[:, :], l)[:, :, 0, :]
                        own(prev)
                    tt(halves(XS[l][:, :], l)[:, :, 0, :], src, decay_to_target(l)).then_inc(pool_scan, 1)
                    if l == 1:
                        tt(halves(xb[:, :], 1)[:, :, 0, :], src, decay_to_target(1)).then_inc(pool_scan, 1)
                    else:
                        if l == 8:
                            pool.wait_ge(dve_proj, after(DVE_PROJ, "ss", u))
                            tt(bn1[:, :], ss[:, :], l2_eps[:, :], ALU.add).then_inc(pool_scan, 1)
                            own("bne")
                            tt(bn2[:, :], bn1[:, :], mhalf[:, :], ALU.pow).then_inc(pool_scan, 1)
                            own("bnp")
                            b_h = beta[:, :, h] if isinstance(h, int) else \
                                beta[:, :, bass.ds(h, 1)].rearrange("p c o -> p (c o)")
                            tt(bn[:, :], bn2[:, :], b_h).then_inc(pool_scan, 1)
                        own(f"x{l}")
                        pool.wait_ge(dve_proj, after(DVE_PROJ, f"f{l}", u))
                        end = halves(F[l][:, :], l)[:, :, 1, l - 1:l].to_broadcast([P, T // (2 * l), l])
                        tt(halves(xb[:, :], l)[:, :, 0, :], halves(XS[l][:, :], l)[:, :, 0, :],
                           end).then_inc(pool_scan, 1)
                    prev = f"b{l}"
                if batch_next is not None:
                    deviation(batch_next)
                pool.wait_ge(act_scan, after(ACT_SCAN, "s0", u))
                prev = None
                for i, l in enumerate(LEVELS[1:]):
                    if l == 64:
                        pool.wait_ge(dve_scan, after(DVE_SCAN, "mst", u))
                        own(prev)
                        tt(s[:, P:T], s[:, P:T], tmp[2][:, :], ALU.add).then_inc(pool_scan, 1)
                        prev = "adst"
                    pool.wait_ge(dve_scan, after(DVE_SCAN, f"m{l}", u))
                    if prev:
                        own(prev)
                    dst = halves(s[:, :], l)[:, :, 1, :]
                    tt(dst, dst, packed(tmp[i % 2][:, 0:T // 2], l), ALU.add).then_inc(pool_scan, 1)
                    prev = f"ad{l}"
                pool.wait_ge(act_scan, after(ACT_SCAN, "aT", u))
                for l in LEVELS[1:]:
                    tt(packed(Y[l][:, :], l), halves(aT[:, :], l)[:, :, 1, :],
                       halves(F[l][:, :], l)[:, :, 1, :]).then_inc(pool_scan, 1)
                tt(Yst[:, :], aT[:, P:T], G[:, P:T]).then_inc(pool_scan, 1)
                pool.wait_ge(dve_scan, after(DVE_SCAN, "rs", u))
                tt(r1[:, :], rs[:, :], rs[:, :]).then_inc(pool_scan, 1)
                own("r1")
                pool.wait_ge(dve_scan, after(DVE_SCAN, "oss", u))
                tt(r2[:, :], r1[:, :], oss[:, :]).then_inc(pool_scan, 1)
                own("r2")
                tt(r3[:, :], r2[:, :], rms_eps[:, :], ALU.add).then_inc(pool_scan, 1)
                own("r3")
                tt(r4[:, :], r3[:, :], mhalf[:, :], ALU.pow).then_inc(pool_scan, 1)
                own("r4")
                tt(r5[:, :], r4[:, :], rs[:, :]).then_inc(pool_scan, 1)

            def batch(b, final):
                with pool.Fori(0, NH - 1) as h:
                    scan(b * NH + h, h)
                scan(b * NH + (NH - 1), NH - 1, None if final else b + 1)

            deviation(0)
            with pool.Fori(0, NB - 1) as b:
                batch(b, False)
            batch(NB - 1, True)

        @block.scalar
        def _(act):
            for steps, done in ((ACT_PROJ, act_proj), (ACT_SCAN, act_scan), (ACT_EDGE, act_edge)):
                act.sem_inc(done, len(steps))
            act.wait_ge(small_full, 16 * SMALL)

            def first_tap(n, unit):
                at = TAP[n] + KW - 1
                if n == "w":
                    act.wait_ge(dve_proj, after(DVE_PROJ, "tap", unit))
                act.wait_ge(pe_proj, after(PE_PROJ, n, unit))
                nc.scalar.activation(acc[n][:, :], bank[n][:, :], ACT.Copy,
                                     scale=tap[:, at:at + 1]).then_inc(act_proj, 1)

            def proj_slots(n, w_read):
                act.wait_ge(dve_proj, after(DVE_PROJ, "cw3", n))
                act.wait_ge(pe_scan, w_read)
                nc.scalar.activation(w[:, :], acc["w"][:, :], ACT.Silu).then_inc(act_proj, 1)
                nc.scalar.activation(xb[:, :], acc["w"][:, :], ACT.Silu).then_inc(act_proj, 1)
                act.wait_ge(dve_proj, after(DVE_PROJ, "ck3", n))
                nc.scalar.activation(k[:, :], acc["k"][:, :], ACT.Silu).then_inc(act_proj, 1)
                act.wait_ge(dve_proj, after(DVE_PROJ, "cv3", n))
                nc.scalar.activation(v[:, :], acc["v"][:, :], ACT.Silu).then_inc(act_proj, 1)

            def proj_decay(n):
                act.wait_ge(pe_proj, after(PE_PROJ, "g", n))
                nc.scalar.activation(g[:, :], bank["g"][:, :], ACT.Sigmoid).then_inc(act_proj, 1)

            def slot_rows(n, sq_read):
                act.wait_ge(pe_proj, after(PE_PROJ, "wT", n))
                act.wait_ge(dve_scan, sq_read)
                nc.scalar.activation(sq[:, :, :], chunks(bank["wT"]), ACT.Square).then_inc(act_proj, 1)
                nc.scalar.activation(XT[0][:, :, :], chunks(bank["wT"]), ACT.Copy).then_inc(act_proj, 1)

            def transposed_rows(b, kk):
                act.wait_ge(pe_edge, after(PE_EDGE, f"lnT{kk}", b))
                nc.scalar.activation(hT[:, kk, :], edge_bank[f"lnT{kk}"][:, :], ACT.Copy).then_inc(act_edge, 1)

            def low_ranks(b):
                act.wait_ge(pe_edge, after(PE_EDGE, "f1", b))
                nc.scalar.activation(f1T[:, :], edge_bank["f1"][:, :], ACT.Copy).then_inc(act_edge, 1)
                act.wait_ge(pe_edge, after(PE_EDGE, "g1", b))
                nc.scalar.activation(g1T[:, :], edge_bank["g1"][:, :], ACT.Copy).then_inc(act_edge, 1)
                act.wait_ge(pe_edge, after(PE_EDGE, "beta", b))
                nc.scalar.activation(beta[:, :, :].rearrange("p c h -> p (c h)"), edge_bank["beta"][:, 0:C * NH],
                                     ACT.Sigmoid).then_inc(act_edge, 1)

            def first_head(n):
                first_tap("w", n)
                first_tap("k", n)
                first_tap("v", n)
                proj_slots(n, before(PE_SCAN, n))
                proj_decay(n)
                first_tap("q", n)
                slot_rows(n, before(DVE_SCAN, n))

            def scan(u, h, more, batch_next=None):
                def pe_done(name):
                    act.wait_ge(pe_scan, after(PE_SCAN, name, u))

                def copy_out(dst, name):
                    pe_done(name)
                    nc.scalar.activation(dst, bank[name][:, :], ACT.Copy).then_inc(act_scan, 1)

                act.wait_ge(pe_proj, after(PE_PROJ, "gate", u))
                act.wait_ge(dve_scan, before(DVE_SCAN, u))
                nc.scalar.activation(sg[:, :], bank["gate"][:, :], ACT.Sigmoid,
                                     bias=tap[:, BIAS:BIAS + 1]).then_inc(act_scan, 1)
                copy_out(XT[1][:, :, :].rearrange("p c n -> p (c n)"), "x1T")
                act.wait_ge(dve_proj, after(DVE_PROJ, "cq3", u))
                nc.scalar.activation(q[:, :], acc["q"][:, :], ACT.Silu).then_inc(act_scan, 1)
                for l in LEVELS[1:]:
                    copy_out(XT[l][:, :, :].rearrange("p c n -> p (c n)"), f"x{l}T")
                if more:
                    first_tap("w", u + 1)
                pe_done("xbT")
                nc.scalar.activation(XTB[:, :, :].rearrange("p c n -> p (c n)"), bank["xbT"][:, 0:T - P],
                                     ACT.Copy).then_inc(act_scan, 1)
                copy_out(s[:, :], "s0")
                pe_done("skT")
                nc.scalar.activation(Sk[:, :, :].rearrange("p c n -> p (c n)"), bank["skT"][:, 0:T - P],
                                     ACT.Copy).then_inc(act_scan, 1)
                if batch_next is not None:
                    for kk in range(KT):
                        transposed_rows(batch_next, kk)
                if more:
                    first_tap("k", u + 1)
                act.wait_ge(dve_scan, after(DVE_SCAN, "nms", u))
                for c in range(C):
                    nc.scalar.activation(au[:, c, :], ck_(bank["sT"], c), ACT.Exp, scale=SCALE, bias=nms[:, c:c + 1],
                                         accum_out=rsum[:, c:c + 1]).then_inc(act_scan, 1)
                copy_out(aT[:, :], "aT")
                if more:
                    first_tap("v", u + 1)
                    proj_slots(u + 1, after(PE_SCAN, "a2d", u))
                if batch_next is not None:
                    low_ranks(batch_next)
                pe_done("o")
                nc.scalar.activation(sq[:, :, :], chunks(bank["o"]), ACT.Square,
                                     scale=P ** -0.5).then_inc(act_scan, 1)
                if more:
                    proj_decay(u + 1)
                    first_tap("q", u + 1)
                    slot_rows(u + 1, after(DVE_SCAN, "oss", u))

            def batch(b, final):
                with act.Fori(0, NH - 1) as h:
                    scan(b * NH + h, h, True)
                scan(b * NH + (NH - 1), NH - 1, False, None if final else b + 1)

            for kk in range(KT):
                transposed_rows(0, kk)
            low_ranks(0)
            first_head(0)
            with act.Fori(0, NB - 1) as b:
                batch(b, False)
                first_head(b * NH + NH)
            batch(NB - 1, True)

        @block.vector
        def _(dve):
            for steps, done in ((DVE_PROJ, dve_proj), (DVE_SCAN, dve_scan), (DVE_EDGE, dve_edge), (DVE_OUT, dve_out)):
                dve.sem_inc(done, len(steps))
            for l in LEVELS:
                nc.vector.memset(XS[l][:, :], 0.0).then_inc(dve_consts, 1)
            nc.vector.memset(F[2][:, :], 1.0).then_inc(dve_consts, 1)
            for l in LEVELS[1:]:
                nc.vector.memset(cc[l][:, :, :], 1.0).then_inc(dve_consts, 1)
            dve.wait_ge(dve_consts, 14)
            dve.wait_ge(pool_consts, 27)
            dve.wait_ge(small_full, 16 * SMALL)

            def conv(n, j, unit):
                if j == 1:
                    dve.wait_ge(act_proj, after(ACT_PROJ, f"acc_{n}", unit))
                else:
                    dve.wait_ge(dve_proj, after(DVE_PROJ, f"c{n}{j - 1}", unit))
                at = TAP[n] + KW - 1 - j
                nc.vector.scalar_tensor_tensor(acc[n][:, j:], bank[n][:, 0:T - j], tap[:, at:at + 1],
                                               acc[n][:, j:], ALU.mult, ALU.add).then_inc(dve_proj, 1)

            def head_taps(n, h):
                src = per_head[:, h, :] if isinstance(h, int) else \
                    per_head[:, bass.ds(h, 1), :].rearrange("p o n -> p (o n)")
                nc.vector.tensor_scalar(tap[:, :], src, 1.0, None, ALU.mult).then_inc(dve_proj, 1)

            def slot_squares(n):
                dve.wait_ge(act_proj, after(ACT_PROJ, "sq", n))
                nc.vector.tensor_reduce(ss[:, :], sq[:, :, :], AX.X, ALU.add).then_inc(dve_proj, 1)

            def block_factor(l, done):
                nc.vector.tensor_tensor(cc[l][:, :, 1:2], halves(F[l][:, :], l)[:, :, 0, l - 1:l],
                                        halves(g[:, :], l)[:, :, 1, 0:1], ALU.mult).then_inc(done, 1)

            def double(l, done):
                whole = cc[l][:, :, :].rearrange("p n (two o) -> p (n two) o", o=1)
                nc.vector.tensor_tensor(packed(F[2 * l][:, :], l), packed(F[l][:, :], l),
                                        whole.to_broadcast([P, T // l, l]), ALU.mult).then_inc(done, 1)

            def f_step(n, name):
                if name == "ss":
                    slot_squares(n)
                elif name[:2] == "cq":
                    conv("q", int(name[2]), n)
                elif name == "f2":
                    dve.wait_ge(act_proj, after(ACT_PROJ, "g", n))
                    nc.vector.tensor_copy(halves(F[2][:, :], 1)[:, :, 1, :],
                                          halves(g[:, :], 1)[:, :, 1, :]).then_inc(dve_proj, 1)
                elif name[0] == "c":
                    dve.wait_ge(dve_proj, after(DVE_PROJ, f"f{name[1:]}", n))
                    block_factor(int(name[1:]), dve_proj)
                else:
                    l = int(name[1:]) // 2
                    dve.wait_ge(dve_proj, after(DVE_PROJ, f"c{l}", n))
                    double(l, dve_proj)

            F_STEPS = DVE_PROJ[DVE_PROJ.index("f2"):]

            def row_stats(b):
                dve.wait_ge(xn_full, (b + 1) * 16)
                for c in range(C):
                    nc.vector.bn_stats(stats[:, c, :], xn[:, c, :]).then_inc(dve_edge, 1)
                dve.wait_ge(dve_edge, after(DVE_EDGE, "st3", b))
                nc.vector.memset(hold[:, :], 0.0)
                for c in range(C):
                    nc.vector.bn_aggr(mv[:, c, :], stats[:, c, :]).then_inc(dve_edge, 1)

            def norm_rows(b, c):
                dve.wait_ge(pool_edge, after(POOL_EDGE, "rstd", b))
                nc.vector.tensor_scalar(xn[:, c, :], xn[:, c, :], mv[:, c, 0:1], rstd[:, c:c + 1],
                                        ALU.subtract, ALU.mult).then_inc(dve_edge, 1)

            def scan(u, h, more, batch_next=None):
                def own(name):
                    dve.wait_ge(dve_scan, after(DVE_SCAN, name, u))

                def pe_done(name):
                    dve.wait_ge(pe_scan, after(PE_SCAN, name, u))

                def tt(out, in0, in1, op=ALU.mult):
                    return nc.vector.tensor_tensor(out, in0, in1, op)

                if batch_next is not None:
                    row_stats(batch_next)
                dve.wait_ge(pool_scan, after(POOL_SCAN, "bn", u))
                pe_done("kT")
                by_step = bn[:, :].rearrange("p (c o) -> p c o", o=1).to_broadcast([P, C, P])
                tt(kv[:, :, 0:P], chunks(bank["kT"]), by_step).then_inc(dve_scan, 1)
                pe_done("A")
                tt(chunks(As), chunks(bank["A"]), by_step).then_inc(dve_scan, 1)
                own("As")
                eye = ident[:, :].rearrange("p (o n) -> p o n", o=1).to_broadcast([P, C, P])
                tt(chunks(AM[0]), chunks(As), eye).then_inc(dve_scan, 1)
                for l in LEVELS:
                    tt(packed(AM[l][:, :], l), halves(As[:, :], l)[:, :, 1, :],
                       packed(mask[l][:, :], l)).then_inc(dve_scan, 1)
                    if l == 2:
                        pe_done("vT")
                        tt(kv[:, :, P:2 * P], chunks(bank["vT"]), by_step).then_inc(dve_scan, 1)

                if more or batch_next is not None:
                    dve.wait_ge(act_scan, after(ACT_SCAN, "sg", u))
                    dve.wait_ge(dve_proj, after(DVE_PROJ, "cq3", u))
                    head_taps(u + 1, h + 1 if more else 0)
                dve.wait_ge(dve_proj, after(DVE_PROJ, "f64", u))
                block_factor(64, dve_scan)
                own("c64")
                double(64, dve_scan)
                own("f128")
                tt(chunks(G), chunks(F[P]), chunks(g)[:, :, 0:1].to_broadcast([P, C, P])).then_inc(dve_scan, 1)

                def level_scores(l):
                    i = LEVELS[1:].index(l)
                    pe_done(f"s{l}")
                    if i >= 2:
                        dve.wait_ge(pool_scan, after(POOL_SCAN, f"ad{LEVELS[1:][i - 2]}", u))
                    tt(packed(tmp[i % 2][:, 0:T // 2], l), packed(bank[f"s{l}"][:, 0:T // 2], l),
                       halves(F[l][:, :], l)[:, :, 1, :]).then_inc(dve_scan, 1)

                def end_state(c):
                    pe_done(f"U{c}")
                    if c:
                        own(f"St{c - 1}")
                        nc.vector.scalar_tensor_tensor(state[:, c, :], state[:, c - 1, :],
                                                       G[:, (c + 1) * P - 1:(c + 1) * P], bank[f"U{c}"][:, 0:2 * P],
                                                       ALU.mult, ALU.add).then_inc(dve_scan, 1)
                    else:
                        own("G")
                        nc.vector.tensor_copy(state[:, 0, :], bank["U0"][:, 0:2 * P]).then_inc(dve_scan, 1)

                def beside(j):
                    if more:
                        conv("w", j, u + 1)
                    if batch_next is not None:
                        norm_rows(batch_next, j - 1)
                        if j == C - 1:
                            norm_rows(batch_next, j)

                level_scores(2)
                end_state(0)
                end_state(1)
                beside(1)
                level_scores(4)
                beside(2)
                end_state(2)
                level_scores(8)
                beside(3)
                level_scores(16)
                level_scores(32)
                pe_done("sst")
                tt(tmp[2][:, :], bank["sst"][:, 0:T - P], G[:, P:T]).then_inc(dve_scan, 1)
                level_scores(64)
                pe_done("sT")
                nc.vector.tensor_reduce(nmx[:, :], chunks(bank["sT"]), AX.X, ALU.max, negate=True).then_inc(dve_scan, 1)
                own("mx")
                nc.vector.tensor_scalar(nms[:, :], nmx[:, :], SCALE, None, ALU.mult).then_inc(dve_scan, 1)
                if more:
                    for j in range(1, KW):
                        conv("k", j, u + 1)
                dve.wait_ge(act_scan, after(ACT_SCAN, "e3", u))
                nc.vector.reciprocal(rs[:, :], rsum[:, :]).then_inc(dve_scan, 1)
                pe_done("a2d")
                tt(chunks(A2), chunks(bank["a2d"]), eye).then_inc(dve_scan, 1)
                own("a2d")
                for l in LEVELS:
                    pe_done(f"a2_{l}")
                    nc.vector.memset(hold[:, :], 0.0)
                    nc.vector.copy_predicated(halves(A2[:, :], l)[:, :, 1, :], packed(mask[l][:, :], l).bitcast(INT32),
                                              packed(bank[f"a2_{l}"][:, 0:T // 2], l)).then_inc(dve_scan, 1)
                    if more and l in (8, 32, 64):
                        conv("v", (8, 32, 64).index(l) + 1, u + 1)
                    own(f"a2_{l}")
                dve.wait_ge(act_scan, after(ACT_SCAN, "osq", u))
                nc.vector.tensor_reduce(oss[:, :], sq[:, :, :], AX.X, ALU.add).then_inc(dve_scan, 1)
                if more:
                    for name in F_STEPS[:3]:
                        f_step(u + 1, name)
                dve.wait_ge(pool_scan, after(POOL_SCAN, "r5", u))
                tt(on[:, :, :], chunks(bank["o"]),
                   r5[:, :].rearrange("p (c o) -> p c o", o=1).to_broadcast([P, C, P])).then_inc(dve_scan, 1)
                if more:
                    for name in F_STEPS[3:5]:
                        f_step(u + 1, name)
                pe_done("onT")
                dst = og[:, h, :] if isinstance(h, int) else og[:, bass.ds(h, 1), :].rearrange("p o t -> p (o t)")
                nc.vector.scalar_tensor_tensor(dst, bank["onT"][:, :], norm_w[:, 0:1], sg[:, :],
                                               ALU.mult, ALU.mult).then_inc(dve_scan, 1)
                if more:
                    for name in F_STEPS[5:]:
                        f_step(u + 1, name)

            def first_convolutions(n):
                for x in "wkv":
                    for j in range(1, KW):
                        conv(x, j, n)
                for name in F_STEPS[:5]:
                    f_step(n, name)

            def residual(b):
                dve.wait_ge(res_full, (b + 1) * 16)
                for c in range(C):
                    dve.wait_ge(pe_out, after(PE_OUT, f"o{c}", b))
                    nc.vector.tensor_tensor(res[:, c, :], out_bank[c][:, :], res[:, c, :],
                                            ALU.add).then_inc(dve_out, 1)

            def batch(b, final):
                with dve.Fori(0, NH - 1) as h:
                    scan(b * NH + h, h, True)
                scan(b * NH + (NH - 1), NH - 1, False, None if final else b + 1)

            row_stats(0)
            for c in range(C):
                norm_rows(0, c)
            head_taps(0, 0)
            first_convolutions(0)
            for name in F_STEPS[5:]:
                f_step(0, name)
            with dve.Fori(0, NB - 1) as b:
                batch(b, False)
                first_convolutions(b * NH + NH)
                residual(b)
                for name in F_STEPS[5:]:
                    f_step(b * NH + NH, name)
            batch(NB - 1, True)
            residual(NB - 1)

        @block.tensor
        def _(pe):
            for steps, done in ((PE_PROJ, pe_proj), (PE_SCAN, pe_scan), (PE_EDGE, pe_edge), (PE_OUT, pe_out)):
                pe.sem_inc(done, len(steps))
            pe.wait_ge(pool_consts, 27)
            pe.wait_ge(small_full, 16 * SMALL)

            def arrived(n, unit):
                pe.wait_ge(slot_full[n], (unit + 1) * 16)

            def project(n, kk):
                mm = nc.tensor.matmul(bank[n][:, :], ck_(slot[n], kk), hT[:, kk, :], start=(kk == 0),
                                      stop=(kk == KT - 1))
                if kk == KT - 1:
                    mm.then_inc(pe_proj, 1)

            def project_decay():
                nc.tensor.matmul(bank["g"][:, :], slot["g"][:, :], f1T[:, :], start=True,
                                 stop=True).then_inc(pe_proj, 1)

            def project_gate(n):
                arrived("gate", n)
                pe.wait_ge(dve_proj, after(DVE_PROJ, "cv3", n))
                nc.tensor.matmul(bank["gate"][:, :], slot["gate"][:, :], g1T[:, :], start=True,
                                 stop=True).then_inc(pe_proj, 1)

            def slot_rows(n):
                pe.wait_ge(act_proj, after(ACT_PROJ, "w", n))
                for c in range(C):
                    last = nc.tensor.transpose(ck_(bank["wT"], c), ck_(w, c), ident[:, :])
                last.then_inc(pe_proj, 1)

            def transpose_rows(b, kk):
                if kk == 0:
                    pe.wait_ge(dve_edge, after(DVE_EDGE, "xn3", b))
                if kk >= 2:
                    pe.wait_ge(act_edge, after(ACT_EDGE, f"hT{kk - 2}", b))
                for c in range(C):
                    last = nc.tensor.transpose(ck_(edge_bank[f"lnT{kk}"], c), xn[:, c, kk * P:(kk + 1) * P],
                                               ident[:, :])
                last.then_inc(pe_edge, 1)

            def low_rank(b, name, wt):
                pe.wait_ge(act_edge, after(ACT_EDGE, "hT3", b))
                for kk in range(KT):
                    last = nc.tensor.matmul(edge_bank[name][:, :], wt[:, kk, :], hT[:, kk, :], start=(kk == 0),
                                            stop=(kk == KT - 1))
                last.then_inc(pe_edge, 1)

            def betas():
                for c in range(C):
                    for kk in range(KT):
                        last = nc.tensor.matmul(edge_bank["beta"][:, c * NH:(c + 1) * NH], ck_(hT[:, kk, :], c),
                                                wb[:, kk, :], start=(kk == 0), stop=(kk == KT - 1))
                last.then_inc(pe_edge, 1)

            def first_w_k(b, n):
                arrived("w", n)
                pe.wait_ge(act_edge, after(ACT_EDGE, "f1", b))
                for kk in range(KT):
                    project("w", kk)
                arrived("k", n)
                pe.wait_ge(act_edge, after(ACT_EDGE, "g1", b))
                for kk in range(KT):
                    project("k", kk)

            def first_v_g(b, n):
                arrived("v", n)
                pe.wait_ge(dve_proj, after(DVE_PROJ, "cw3", n))
                for kk in range(KT):
                    project("v", kk)
                arrived("g", n)
                pe.wait_ge(act_edge, after(ACT_EDGE, "beta", b))
                project_decay()

            def first_q(n):
                arrived("q", n)
                pe.wait_ge(dve_proj, after(DVE_PROJ, "ck3", n))
                for kk in range(KT):
                    project("q", kk)
                project_gate(n)
                slot_rows(n)

            def scan(u, more, batch_next=None):
                def act_done(name):
                    pe.wait_ge(act_scan, after(ACT_SCAN, name, u))

                def dve_done(name):
                    pe.wait_ge(dve_scan, after(DVE_SCAN, name, u))

                def pool_done(name):
                    pe.wait_ge(pool_scan, after(POOL_SCAN, name, u))

                def transpose(name, src, n=C):
                    for c in range(n):
                        last = nc.tensor.transpose(ck_(bank[name], c), src(c), ident[:, :])
                    last.then_inc(pe_scan, 1)

                def fill(*parts):
                    if more:
                        for n, kk in parts:
                            if kk == 0:
                                arrived(n, u + 1)
                                if n == "w":
                                    act_done("sg")
                                if n == "k":
                                    pe.wait_ge(dve_proj, after(DVE_PROJ, "cq3", u))
                                if n == "v":
                                    pe.wait_ge(dve_proj, after(DVE_PROJ, "cw3", u + 1))
                                if n == "q":
                                    pe.wait_ge(dve_proj, after(DVE_PROJ, "ck3", u + 1))
                            project(n, kk)

                def scores(l):
                    for c in range(C):
                        last = nc.tensor.matmul(ck_(bank[f"s{l}"], c, P // 2), XT[l][:, c, :],
                                                ck_(AM[l], c, P // 2), start=True, stop=True)
                    last.then_inc(pe_scan, 1)

                pe.wait_ge(act_proj, after(ACT_PROJ, "k", u))
                transpose("kT", lambda c: ck_(k, c))
                pe.wait_ge(dve_scan, before(DVE_SCAN, u))
                pool_done("x1")
                transpose("x1T", lambda c: ck_(XS[1], c))
                pool_done("x2")
                pe.wait_ge(act_proj, after(ACT_PROJ, "xt0", u))
                transpose("x2T", lambda c: ck_(XS[2], c))
                fill(("w", 0))
                pool_done("x4")
                act_done("xt1")
                transpose("x4T", lambda c: ck_(XS[4], c))
                fill(("w", 1))
                act_done("q")
                for c in range(C):
                    last = nc.tensor.matmul(ck_(bank["A"], c), ck_(k, c), ck_(q, c), start=True, stop=True)
                last.then_inc(pe_scan, 1)
                pool_done("x8")
                act_done("xt2")
                transpose("x8T", lambda c: ck_(XS[8], c))
                pool_done("x16")
                act_done("xt4")
                transpose("x16T", lambda c: ck_(XS[16], c))
                fill(("w", 2))
                pool_done("x32")
                act_done("xt8")
                transpose("x32T", lambda c: ck_(XS[32], c))
                act_done("xt16")
                transpose("vT", lambda c: ck_(v, c))
                fill(("w", 3))
                pool_done("x64")
                act_done("xt32")
                transpose("x64T", lambda c: ck_(XS[64], c))
                pool_done("b64")
                dve_done("vr")
                transpose("xbT", lambda c: ck_(xb, c), C - 1)
                dve_done("am1")
                for c in range(C):
                    nc.tensor.matmul(ck_(bank["s0"], c), XT[0][:, c, :], ck_(AM[0], c), start=True, stop=False)
                    last = nc.tensor.matmul(halves(ck_(bank["s0"], c), 1)[:, :, 1, 0], XT[1][:, c, :],
                                            ck_(AM[1], c, P // 2), start=False, stop=True)
                last.then_inc(pe_scan, 1)
                dve_done("am2")
                scores(2)
                def chunk_adds(c):
                    nc.tensor.matmul(bank[f"U{c}"][:, 0:2 * P], XTB[:, c, :], kv[:, c, :], start=True,
                                     stop=True).then_inc(pe_scan, 1)

                act_done("xtb")
                chunk_adds(0)
                chunk_adds(1)
                dve_done("am4")
                act_done("s0")
                scores(4)
                dve_done("m2")
                scores(8)
                dve_done("St0")
                chunk_adds(2)
                dve_done("m4")
                scores(16)
                dve_done("St2")
                act_done("xt64")
                transpose("skT", lambda c: state[:, c, 0:P], C - 1)
                dve_done("m8")
                scores(32)
                act_done("sk")
                if batch_next is not None:
                    act_done("sg")
                    transpose_rows(batch_next, 0)
                    pe.wait_ge(dve_proj, after(DVE_PROJ, "cq3", u))
                    transpose_rows(batch_next, 1)
                dve_done("m16")
                for c in range(C - 1):
                    last = nc.tensor.matmul(ck_(bank["sst"], c), Sk[:, c, :], ck_(q, c + 1), start=True, stop=True)
                last.then_inc(pe_scan, 1)
                dve_done("m32")
                scores(64)
                fill(("k", 0), ("k", 1), ("k", 2), ("k", 3))
                if batch_next is not None:
                    transpose_rows(batch_next, 2)
                    transpose_rows(batch_next, 3)
                pool_done("ad64")
                transpose("sT", lambda c: ck_(s, c))
                fill(("v", 0), ("v", 1), ("v", 2))
                if batch_next is not None:
                    low_rank(batch_next, "f1", wf1)
                act_done("e3")
                transpose("aT", lambda c: au[:, c, :])
                fill(("v", 3))
                if batch_next is not None:
                    low_rank(batch_next, "g1", wg1)
                act_done("aT")
                for c in range(C):
                    last = nc.tensor.matmul(ck_(bank["a2d"], c), ck_(w, c), ck_(aT, c), start=True, stop=True)
                last.then_inc(pe_scan, 1)
                for c in range(C):
                    last = nc.tensor.matmul(ck_(bank["a2_1"], c, P // 2), ck_(XS[1], c),
                                            halves(ck_(aT, c), 1)[:, :, 1, 0], start=True, stop=True)
                last.then_inc(pe_scan, 1)
                for l in LEVELS[1:]:
                    pool_done(f"y{l}")
                    dve_done("a2d" if l == 2 else f"a2_{l // 4}")
                    for c in range(C):
                        last = nc.tensor.matmul(ck_(bank[f"a2_{l}"], c, P // 2), ck_(XS[l], c),
                                                ck_(Y[l], c, P // 2), start=True, stop=True)
                    last.then_inc(pe_scan, 1)
                if more:
                    arrived("g", u + 1)
                    project_decay()
                if batch_next is not None:
                    betas()
                dve_done("a2_64")
                pool_done("yst")
                for c in range(C):
                    last = nc.tensor.matmul(ck_(bank["o"], c), ck_(A2, c), kv[:, c, P:2 * P], start=True, stop=(c == 0))
                    if c:
                        last = nc.tensor.matmul(ck_(bank["o"], c), ck_(Yst, c - 1), state[:, c - 1, P:2 * P],
                                                start=False, stop=True)
                last.then_inc(pe_scan, 1)
                fill(("q", 0), ("q", 1), ("q", 2), ("q", 3))
                if more:
                    project_gate(u + 1)
                    slot_rows(u + 1)
                if batch_next is not None:
                    first_w_k(batch_next, u + 1)
                dve_done("on")
                transpose("onT", lambda c: on[:, c, :])

            def head_rows(b, h):
                pe.wait_ge(wo_full[h % 4], b * (16 * NH // 4) + 16 * (h // 4 + 1))
                for c in range(C):
                    last = nc.tensor.matmul(out_bank[c][:, :], ck_(og[:, h, :], c), wo[h % 4][:, :],
                                            start=(h == 0), stop=(h == NH - 1))
                    if h == NH - 1:
                        last.then_inc(pe_out, 1)
                if h < NH - 1:
                    last.then_inc(pe_out, 1)

            for kk in range(KT):
                transpose_rows(0, kk)
            low_rank(0, "f1", wf1)
            low_rank(0, "g1", wg1)
            betas()
            first_w_k(0, 0)
            first_v_g(0, 0)
            first_q(0)
            with pe.Fori(0, NB - 1) as b:
                with pe.Fori(0, NH - 1) as h:
                    scan(b * NH + h, True)
                scan(b * NH + (NH - 1), False, b + 1)
                pe.wait_ge(dve_scan, before(DVE_SCAN, (b + 1) * NH))
                for h in range(NH // 2):
                    head_rows(b, h)
                first_v_g(b + 1, b * NH + NH)
                for h in range(NH // 2, NH):
                    head_rows(b, h)
                first_q(b * NH + NH)
                pe.wait_ge(dve_out, before(DVE_OUT, b + 1))
            b = NB - 1
            with pe.Fori(0, NH - 1) as h:
                scan(b * NH + h, True)
            scan(b * NH + (NH - 1), False)
            pe.wait_ge(dve_scan, before(DVE_SCAN, (b + 1) * NH))
            for h in range(NH):
                head_rows(b, h)


def build(nc, a, out):
    x1 = nc.dram_tensor("x1", (NB * T, HID), FP32, kind="Internal").ap()
    x2 = nc.dram_tensor("x2", (NB * T, HID), FP32, kind="Internal").ap()
    wq_dram = nc.dram_tensor("wq_dram", (3, P, KT * FF), FP32, kind="Internal").ap()
    ffn_w = (a["w1"], a["w2"], a["w3"])
    ffn_phase(nc, True, a["x"], x1, ffn_w, wq_dram)
    attention_phase(nc, x1, x2, a)
    ffn_phase(nc, False, x2, out, ffn_w, wq_dram)


def kernel(**inputs):
    import numpy as _np
    import concourse.bacc as _bacc
    from concourse import mybir as _mybir
    from concourse.bass_utils import run_bass_kernel_spmd as _run

    a = {k[3:]: _np.asarray(v) for k, v in inputs.items()}

    def heads_first(w):
        k = w.shape[0] // 128
        return w.reshape(k, 128, 16, 128).transpose(2, 1, 0, 3).reshape(16, 128, k * 128)

    def channels(w):
        return w.reshape(16, 128, -1).transpose(1, 0, 2)

    laid = {
        "x": a["attn_hidden_states"].reshape(2048, 512),
        "wq": heads_first(a["attn_Wq"]), "wk": heads_first(a["attn_Wk"]),
        "wv": heads_first(a["attn_Wv"]), "ww": heads_first(a["attn_Ww"]),
        "wf2": heads_first(a["attn_Wf2"]), "wg2": heads_first(a["attn_Wg2"]),
        "per_head": _np.concatenate([channels(a[f"attn_{n}"]) for n in ("cq", "ck", "cv", "bg2")], axis=2),
        "norm_w": a["attn_norm_w"].reshape(128, 1),
        "wf1": a["attn_Wf1"], "wg1": a["attn_Wg1"], "wb": a["attn_Wb"],
        "wo": a["attn_Wo"].reshape(16, 128, 512),
        "w1": a["ffn_w1"].T, "w2": a["ffn_w2"].T, "w3": a["ffn_w3"].T,
    }
    nc = _bacc.Bacc("TRN2", target_bir_lowering=False, num_devices=1)
    arrays, args = {}, {}
    for name, v in laid.items():
        v = _np.ascontiguousarray(v)
        arrays[f"in_{name}_dram"] = v
        args[name] = nc.dram_tensor(f"in_{name}_dram", v.shape, _mybir.dt.from_np(v.dtype), kind="ExternalInput").ap()
    out = nc.dram_tensor("out_dram", (2048, 512), _mybir.dt.float32, kind="ExternalOutput").ap()
    build(nc, args, out)
    r = _run(nc, [arrays], core_ids=[0])
    return r.results[0]["out_dram"].reshape(4, 512, 512)
```
